# Optimizing a Trainium2 kernel written in Bass

```python
import numpy as np
import jax
import jax.numpy as jnp

def _softmax(x, axis=-1):
    return jax.nn.softmax(x, axis=axis)

def _gelu(x):
    return jax.nn.gelu(x, approximate=True)

def _silu(x):
    return jax.nn.silu(x)

def _sigmoid(x):
    return jax.nn.sigmoid(x)

def _layernorm(x, axis=-1, eps=1e-05):
    m = jnp.mean(x, axis=axis, keepdims=True)
    v = jnp.var(x, axis=axis, keepdims=True)
    return (x - m) / jnp.sqrt(v + eps)

def _scatter_add(tgt, idx, src, axis=0):
    return tgt.at[idx].add(src)

def _segment_sum(src, seg, n):
    return jax.ops.segment_sum(src, seg, n)
kernel_name = 'mk_adj_preln_d2_adj_r2_a67b18'

def setup_inputs(seed: int=0):
    np.random.seed(seed)
    _w = jnp.asarray

    def _rec_inputs():
        import jax
        import jax.numpy as jnp
        _gk = jax.random.key(seed)
        x = -4.645e-05 + 0.05002 * jax.random.normal(jax.random.fold_in(_gk, 1), (4096, 128), jnp.float32)
        _w = (1.0 + jnp.arange(4096, dtype=jnp.float32)) ** (-0.5)
        _w = _w / _w.mean()
        _pij = jnp.clip(0.00390625 * _w[:, None] * _w[None, :], 0.0, 1.0)
        _a = jax.random.uniform(jax.random.fold_in(_gk, 2), (4096, 4096)) < _pij
        _af = _a.astype(jnp.float32)
        _af = _af / jnp.maximum(_af.sum(-1, keepdims=True), 1.0)
        adj = _af
        return (x, adj)
    x, adj = _rec_inputs()

    def _L0_gnn_setup():
        import jax, jax.numpy as jnp
        import numpy as np
        EPS = 1e-07
        MAX_TANH = 1.0 - 1e-06

        def _norm(v):
            return jnp.maximum(jnp.linalg.norm(v, axis=-1, keepdims=True), EPS)

        def log_map_zero(y):
            n = _norm(y)
            return jnp.arctanh(jnp.clip(n, 0.0, MAX_TANH)) * y / n

        def exp_map_zero(v):
            n = _norm(v)
            return jnp.tanh(n) * v / n

        def h_add(x, y):
            xy = jnp.sum(x * y, axis=-1, keepdims=True)
            x2 = jnp.sum(x * x, axis=-1, keepdims=True)
            y2 = jnp.sum(y * y, axis=-1, keepdims=True)
            num = (1.0 + 2.0 * xy + y2) * x + (1.0 - x2) * y
            den = 1.0 + 2.0 * xy + x2 * y2
            return num / jnp.maximum(den, EPS)

        def h_mul(x, W):
            return exp_map_zero(log_map_zero(x) @ W)
        key = jax.random.key(seed)
        k1, k2, k3, k4 = jax.random.split(key, 4)
        N, F_IN, F_OUT = (4096, 128, 128)
        x = 0.05 * jax.random.normal(k1, (N, F_IN), dtype=jnp.float32)
        a = (jax.random.uniform(k2, (N, N)) < 0.01).astype(jnp.float32)
        adj = a / jnp.maximum(a.sum(axis=1, keepdims=True), 1.0)
        lim_e = np.sqrt(6.0 / (F_IN + F_IN)) * np.sqrt(2.0)
        lim_l = np.sqrt(6.0 / (2 * F_IN + F_OUT)) * np.sqrt(2.0)
        embed = jax.random.uniform(k3, (F_IN, F_IN), minval=-lim_e, maxval=lim_e, dtype=jnp.float32)
        layer = jax.random.uniform(k4, (2 * F_IN, F_OUT), minval=-lim_l, maxval=lim_l, dtype=jnp.float32)
        embed_bias = jnp.zeros((F_IN,), dtype=jnp.float32)
        layer_bias = jnp.zeros((F_OUT,), dtype=jnp.float32)
        return {'x': x, 'adj': adj, 'embed': embed, 'layer': layer, 'embed_bias': embed_bias, 'layer_bias': layer_bias}
    _L0_gnn_all = _L0_gnn_setup()
    _L0_gnn_in = {k: v for k, v in _L0_gnn_all.items() if k in ('embed', 'layer', 'embed_bias', 'layer_bias')}
    del _L0_gnn_all

    def _L1_gnn_setup():
        import jax, jax.numpy as jnp
        import numpy as np
        N = 4096
        F = 128
        AVG_DEGREE = 32
        NEG_INF = -1000000000.0
        LEAKY_ALPHA = 0.3
        EPS = 1e-12

        def _agnn(x, a, beta):
            x_norm = x / jnp.clip(jnp.linalg.norm(x, axis=-1, keepdims=True), EPS, None)
            scores = beta[0] * (x_norm @ x_norm.T)
            scores = jnp.where(a > 0, scores, NEG_INF)
            attn = jax.nn.softmax(scores, axis=-1)
            return attn @ x

        def _leaky(h):
            return jnp.where(h > 0, h, LEAKY_ALPHA * h)
        key = jax.random.key(seed)
        k1, k2 = jax.random.split(key)
        x = jax.random.normal(k1, (N, F), dtype=jnp.float32)
        a = (jax.random.uniform(k2, (N, N)) < AVG_DEGREE / N).astype(jnp.float32)
        a = jnp.maximum(a, jnp.eye(N, dtype=jnp.float32))
        beta1 = jnp.ones((1,), dtype=jnp.float32)
        beta2 = jnp.ones((1,), dtype=jnp.float32)
        return {'x': x, 'a': a, 'beta1': beta1, 'beta2': beta2}
    _L1_gnn_all = _L1_gnn_setup()
    _L1_gnn_in = {k: v for k, v in _L1_gnn_all.items() if k in ('beta1', 'beta2')}
    del _L1_gnn_all
    return {'x': x, 'adj': adj, 'L0_gnn_embed': _L0_gnn_in['embed'], 'L0_gnn_layer': _L0_gnn_in['layer'], 'L0_gnn_embed_bias': _L0_gnn_in['embed_bias'], 'L0_gnn_layer_bias': _L0_gnn_in['layer_bias'], 'L1_gnn_beta1': _L1_gnn_in['beta1'], 'L1_gnn_beta2': _L1_gnn_in['beta2']}

def reference(x, adj, L0_gnn_embed, L0_gnn_layer, L0_gnn_embed_bias, L0_gnn_layer_bias, L1_gnn_beta1, L1_gnn_beta2):
    import jax
    import jax.numpy as jnp

    def _L0_gnn_ref(x, adj, embed, layer, embed_bias, layer_bias):
        import jax, jax.numpy as jnp
        import numpy as np
        EPS = 1e-07
        MAX_TANH = 1.0 - 1e-06

        def _norm(v):
            return jnp.maximum(jnp.linalg.norm(v, axis=-1, keepdims=True), EPS)

        def log_map_zero(y):
            n = _norm(y)
            return jnp.arctanh(jnp.clip(n, 0.0, MAX_TANH)) * y / n

        def exp_map_zero(v):
            n = _norm(v)
            return jnp.tanh(n) * v / n

        def h_add(x, y):
            xy = jnp.sum(x * y, axis=-1, keepdims=True)
            x2 = jnp.sum(x * x, axis=-1, keepdims=True)
            y2 = jnp.sum(y * y, axis=-1, keepdims=True)
            num = (1.0 + 2.0 * xy + y2) * x + (1.0 - x2) * y
            den = 1.0 + 2.0 * xy + x2 * y2
            return num / jnp.maximum(den, EPS)

        def h_mul(x, W):
            return exp_map_zero(log_map_zero(x) @ W)
        h = h_mul(x, embed)
        h = h_add(h, embed_bias[None, :])
        neigh = exp_map_zero(adj @ log_map_zero(h))
        out = h_mul(jnp.concatenate((x, neigh), axis=1), layer)
        out = h_add(out, layer_bias[None, :])
        return out

    def _L1_gnn_ref(x, a, beta1, beta2):
        import jax, jax.numpy as jnp
        import numpy as np
        N = 4096
        F = 128
        AVG_DEGREE = 32
        NEG_INF = -1000000000.0
        LEAKY_ALPHA = 0.3
        EPS = 1e-12

        def _agnn(x, a, beta):
            x_norm = x / jnp.clip(jnp.linalg.norm(x, axis=-1, keepdims=True), EPS, None)
            scores = beta[0] * (x_norm @ x_norm.T)
            scores = jnp.where(a > 0, scores, NEG_INF)
            attn = jax.nn.softmax(scores, axis=-1)
            return attn @ x

        def _leaky(h):
            return jnp.where(h > 0, h, LEAKY_ALPHA * h)
        h = _leaky(_agnn(x, a, beta1))
        h = _leaky(_agnn(h, a, beta2))
        return h
    h = jnp.maximum(_layernorm(x, axis=-1), 0.0)
    x = x + _L0_gnn_ref(h, adj, L0_gnn_embed, L0_gnn_layer, L0_gnn_embed_bias, L0_gnn_layer_bias)
    h = jnp.maximum(_layernorm(x, axis=-1), 0.0)
    x = x + _L1_gnn_ref(h, adj, L1_gnn_beta1, L1_gnn_beta2)
    return x

_drawn_inputs = setup_inputs


def setup_inputs(seed=0):
    import zlib

    import numpy as np

    out = dict(_drawn_inputs(seed))
    spreads = {'L0_gnn_embed_bias': (0.0, 0.1), 'L0_gnn_layer_bias': (0.0, 0.1)}
    factors = {}
    for name, (base, spread) in spreads.items():
        noise = np.random.default_rng([zlib.crc32(name.encode()), seed]).standard_normal(out[name].shape)
        drawn = base * np.exp(spread * noise) if base else spread * noise
        out[name] = jnp.asarray(drawn.astype(out[name].dtype))
    for name, factor in factors.items():
        out[name] = (out[name] * factor).astype(out[name].dtype)
    return out
```

```python
import numpy as np
import concourse.bass as bass
import concourse.mybir as mybir
from contextlib import ExitStack


def build(nc, x, adj, adj_t, embed, layer, embed_bias, layer_bias, beta1, beta2, out):
    f32, f16, i32 = mybir.dt.float32, mybir.dt.float16, mybir.dt.int32
    ACT, ALU, AX = mybir.ActivationFunctionType, mybir.AluOpType, mybir.AxisListType
    ts, ds = bass.ts, bass.ds

    N, F = x.shape
    P = 128
    NB = N // P
    CH = 512
    CB = CH // P
    NC = N // CH
    TB = 4
    NT = NB // TB
    SB = 2
    NS = NB // SB
    ER = 2
    LAG = 4
    XT = min(NS // 2, NS - 1) if NS > 8 else NS - 1
    AW = 2 * F + 1
    HB = NB // 2
    EPS, MAX_TANH, LN_EPS, NORM_EPS, LEAK = 1e-7, 1.0 - 1e-6, 1e-5, 1e-12, 0.3
    TINY = 1e-30
    FS = 256.0
    P_LOG = 15 * float(np.log(2.0))
    BETA_MAX = 4.0
    SERIES = 0.25

    ctx = ExitStack()
    with ctx:
        def sb(name, shape, dt=f32):
            return ctx.enter_context(nc.sbuf_tensor(name, shape, dt))

        def sem(name):
            return ctx.enter_context(nc.semaphore(name))

        ring = sb("ring", [P, NT, TB, CH])
        x_sb = sb("x_sb", [P, NB, F])
        h_all = sb("h_all", [P, max(NB * F, LAG * SB * CH)])
        h_sb = h_all[:, 0:NB * F].rearrange("p (b f) -> p b f", f=F)
        p_rings = h_all[:, 0:LAG * SB * CH].bitcast(f16).rearrange("p (s r n) -> p s r n", s=2, r=LAG)
        ph_ring, pl_ring = p_rings[:, 0], p_rings[:, 1]
        set1 = sb("set1", [P, 2 * NB * F + NB])
        v_sb = set1[:, 0:NB * F].rearrange("p (b f) -> p b f", f=F)
        h1_sb = set1[:, NB * F:2 * NB * F].rearrange("p (b f) -> p b f", f=F)
        set1_h = set1[:, :].bitcast(f16)
        src0 = sb("src0", [P, NB, AW], f16)
        xt0 = sb("xt0", [F, 2, N], f16)
        src = [src0, set1_h[:, 2 * N:2 * N + NB * AW].rearrange("p (b w) -> p b w", w=AW)]
        xt = [xt0, set1_h[:, 0:2 * N].rearrange("p (s n) -> p s n", s=2)]

        work = sb("work", [P, (ER + LAG) * SB * CH])
        e_ring = work[:, 0:ER * SB * CH].rearrange("p (r n) -> p r n", r=ER)
        m_ring = work[:, ER * SB * CH:(ER + LAG) * SB * CH].rearrange("p (r n) -> p r n", r=LAG)
        adj_rows = work[:, 0:N]
        scr_a = work[:, 0:NB * F].rearrange("p (b f) -> p b f", f=F)
        scr_b = xt0[:, :, :].rearrange("p s n -> p (s n)").bitcast(f32)[:, 0:NB * F].rearrange("p (b f) -> p b f", f=F)
        accs = sb("accs", [P, CB, AW])
        fallback = sb("fallback", [P, AW])
        t1 = sb("t1", [P, CB, F])
        t2 = sb("t2", [P, CB, F])
        t3 = sb("t3", [P, CB, F])
        at_sb = accs[:, :, :].rearrange("p b w -> p (b w)")[:, 0:CH]
        at_sq = accs[:, :, :].rearrange("p b w -> p (b w)")[:, CH:2 * CH]

        w1 = sb("w1", [F, 2 * F])
        w2 = sb("w2", [F, F])
        eb = sb("eb", [P, F])
        lb = sb("lb", [P, F])
        bsq = sb("bsq", [P, F])
        y2 = sb("y2", [P, 2])
        beta = sb("beta", [P, 2])
        beta_abs = sb("beta_abs", [P, 2])
        beta_big = sb("beta_big", [P, 2], i32)
        beta_scale = sb("beta_scale", [P, 2])
        beta_bias = sb("beta_bias", [P, 2])
        beta_sign = sb("beta_sign", [P, 2])
        beta_nsign = sb("beta_nsign", [P, 2])
        p_log = sb("p_log", [P, 1])
        ident = sb("ident", [P, P])
        ones = sb("ones", [P, P])
        ones_h = sb("ones_h", [P, P], f16)
        small = sb("small", [P, 16, HB])
        hh = sb("hh", [P, NB])
        zero = sb("zero", [P, CB])
        neg_t = sb("neg_t", [NB, P])
        neg_rows = sb("neg_rows", [NB, CB, P])
        ext = sb("ext", [P, NB])
        ext8 = sb("ext8", [P, NC])

        s_ps = ctx.enter_context(nc.psum_tensor("s_ps", [P, 2, SB * CH], f32))
        acc_ps = ctx.enter_context(nc.psum_tensor("acc_ps", [P, CB, 512], f32))
        g_ps = s_ps[:, 0, 0:CH].rearrange("p (b f) -> p b f", f=F)
        h1_ps = s_ps[:, 0, CH:2 * CH].rearrange("p (b f) -> p b f", f=F)
        w_ps = s_ps[:, 0, 0:CH].rearrange("p (b f) -> p b f", f=F)
        xt_ps = s_ps[:, 1, 0:CH]
        ht_ps = acc_ps[:, 3, :]
        n_ps = acc_ps[:, 2, 0:CB]

        x_in = [sem(f"x_in{i}") for i in range(2)]
        weights_in = sem("weights_in")
        consts_made = sem("consts_made")
        tile_in = [sem(f"tile_in{k}") for k in range(NT)]
        agg_tiles = sem("agg_tiles")
        vec = sem("vec")
        asked = sem("asked")
        told = sem("told")
        flags = sem("flags")
        h_ready = sem("h_ready")
        ht_done = sem("ht_done")
        ht_copied = sem("ht_copied")
        gh_done = sem("gh_done")
        g_copied = sem("g_copied")
        h1_copied = sem("h1_copied")
        v_ready = sem("v_ready")
        at_ready = sem("at_ready")
        w_done = sem("w_done")
        w_read = sem("w_read")
        xn_ready = [sem(f"xn_ready{i}") for i in range(2)]
        xt_done = [sem(f"xt_done{i}") for i in range(2)]
        xt_hi = [sem(f"xt_hi{i}") for i in range(2)]
        xt_lo = [sem(f"xt_lo{i}") for i in range(2)]
        s_done = [sem(f"s_done{i}") for i in range(2)]
        exp_done = [sem(f"exp_done{i}") for i in range(2)]
        mask_done = [sem(f"mask_done{i}") for i in range(2)]
        ph_done = [sem(f"ph_done{i}") for i in range(2)]
        pl_done = [sem(f"pl_done{i}") for i in range(2)]
        pv_done = [sem(f"pv_done{i}") for i in range(2)]
        acc_out = [sem(f"acc_out{i}") for i in range(2)]
        sums_done = [sem(f"sums_done{i}") for i in range(2)]
        sums_out = [sem(f"sums_out{i}") for i in range(2)]
        clamped = [sem(f"clamped{i}") for i in range(2)]
        rows_in = [sem(f"rows_in{i}") for i in range(2)]
        rows_used = [sem(f"rows_used{i}") for i in range(2)]
        sm_done = [sem(f"sm_done{i}") for i in range(2)]
        sm_read = [sem(f"sm_read{i}") for i in range(2)]
        neg_done = [sem(f"neg_done{i}") for i in range(2)]
        neg_ready = [sem(f"neg_ready{i}") for i in range(2)]
        shift_ready = [sem(f"shift_ready{i}") for i in range(2)]
        max_step = [sem(f"max_step{i}") for i in range(2)]
        out_ready = sem("out_ready")
        stored = sem("stored")

        adj_tiles = adj_t.rearrange("(t b p) i -> t p b i", b=TB, p=P)
        x_v = x.rearrange("(b p) f -> p b f", p=P)
        out_v = out.rearrange("(b p) f -> p b f", p=P)
        adj_v = adj.rearrange("(b p) j -> b p j", p=P)

        def wait(eng, s, value):
            if not isinstance(value, int) or value > 0:
                eng.wait_ge(s, value)

        class Chain:
            def __init__(self, eng, s):
                self.eng, self.s, self.base, self.n = eng, s, 0, 0

            def __call__(self, ins):
                ins.then_inc(self.s, 1)
                self.n += 1
                self.eng.wait_ge(self.s, self.base + self.n)

        def over_f(ap):
            return ap.unsqueeze(2).to_broadcast([P, ap.shape[1], F])

        def over_b(ap, b):
            return ap.unsqueeze(1).to_broadcast([P, b, F])

        ASKS_FIRST, ASKS_HALF, ASKS_CHUNK = 0, 7, 8
        block = ctx.enter_context(nc.Block())

        @block.sync
        def _(sp):
            for i in range(2):
                sp.dma_start(x_sb[:, ts(i, HB), :], x_v[:, ts(i, HB), :]).then_inc(x_in[i], 16)

            def load(k, c):
                sp.dma_start(ring[:, k, :, :], adj_tiles[k, :, :, ds(c * CH, CH)]).then_inc(tile_in[k], 16)

            for k in range(NT):
                load(k, 0)
            with sp.Fori(1, NC) as c:
                for k in range(NT):
                    sp.wait_ge(agg_tiles, (c - 1) * NT + (k + 1))
                    load(k, c)
            for la in range(2):
                for k in range(NT):
                    if la == 0:
                        sp.wait_ge(agg_tiles, (NC - 1) * NT + (k + 1))
                    else:
                        sp.wait_ge(mask_done[0], (NC - 1) * NS + 2 * k + 2)
                    load(k, 0)
                with sp.Fori(1, NC) as c:
                    for k in range(NT):
                        sp.wait_ge(mask_done[la], (c - 1) * NS + (2 * k + 2))
                        load(k, c)

        @block.gpsimd
        def _(pool):
            pool.memset(ident[:, :], 0.0).then_inc(consts_made, 1)
            pool.memset(ones[:, :], 1.0).then_inc(consts_made, 1)
            pool.memset(ones_h[:, :], 1.0).then_inc(consts_made, 1)
            pool.memset(src[0][:, :, 2 * F:AW], FS).then_inc(consts_made, 1)
            pool.memset(p_log[:, :], P_LOG).then_inc(consts_made, 1)
            pool.wait_ge(consts_made, 5)
            pool.affine_select(out=ident[:, :], in_=ident[:, :], compare_op=ALU.not_equal, fill=1.0,
                               base=0, pattern=[[-1, P]], channel_multiplier=1).then_inc(consts_made, 1)
            pool.wait_ge(xn_ready[0], NC)
            pool.wait_ge(agg_tiles, NC * NT)
            pool.memset(src[1][:, :, 2 * F:AW], FS).then_inc(consts_made, 1)
            pool.wait_ge(flags, 1)
            for la in range(2):
                with pool.If(pool.value_load(beta_big[0:1, la:la + 1]) != 0):
                    if la == 0:
                        pool.wait_ge(xt_lo[0], NC)
                    else:
                        pool.wait_ge(pl_done[0], NC * NS)
                        pool.wait_ge(ph_done[0], NC * NS)
                    pool.dma_start(adj_rows, adj_v[0, :, :]).then_inc(rows_in[la], 16)
                    with pool.Fori(1, NB) as b:
                        pool.wait_ge(rows_used[la], b)
                        pool.dma_start(adj_rows, adj_v[ds(b, 1), :, :].rearrange("o p j -> p (o j)"))\
                            .then_inc(rows_in[la], 16)
            with pool.Fori(0, NC) as c:
                pool.wait_ge(out_ready, c + 1)
                pool.dma_start(out_v[:, ds(c * CB, CB), :], x_sb[:, ds(c * CB, CB), :]).then_inc(stored, 16)
            pool.wait_ge(stored, 16 * NC)

        @block.tensor
        def _(pe):
            pe.wait_ge(consts_made, 6)
            pe.wait_ge(weights_in, 16 * 7)

            for r in range(NC):
                pe.wait_ge(h_ready, 1 + r // (NC // 2))
                wait(pe, ht_copied, r)
                for b in range(CB):
                    last = nc.tensor.transpose(ht_ps[:, ts(b, P)], h_sb[:, r * CB + b, :], ident[:, :])
                last.then_inc(ht_done, 1)
                pe.wait_ge(ht_copied, r + 1)
                wait(pe, g_copied, r)
                wait(pe, h1_copied, r)
                for b in range(CB):
                    nc.tensor.matmul(g_ps[:, b, :], at_sb[:, ts(b, P)], w1[:, 0:F], start=True, stop=True)
                    last = nc.tensor.matmul(h1_ps[:, b, :], at_sb[:, ts(b, P)], w1[:, F:2 * F],
                                            start=True, stop=True)
                last.then_inc(gh_done, 1)

            def layer_product():
                for b in range(CB):
                    nc.tensor.matmul(w_ps[:, b, :], at_sb[:, ts(b, P)], w2[:, :], start=True, stop=True)
                for b in range(CB):
                    last = nc.tensor.matmul(n_ps[:, b:b + 1], at_sq[:, ts(b, P)], ones[:, 0:1],
                                            start=True, stop=True)
                last.then_inc(w_done, 1)

            def transposes(la, out_ps):
                for b in range(CB):
                    last = nc.tensor.transpose(out_ps[:, ts(b, P)], t3[:, b, :], ident[:, :])
                last.then_inc(xt_done[la], 1)

            def aggregate(c, parity, prev, prev2):
                agg = acc_ps[:, parity, :]
                for k in range(NT):
                    pe.wait_ge(tile_in[k], 16 * c + 16)
                    if prev2 and k == 0:
                        wait(pe, at_ready, c - 1)
                    for b in range(TB):
                        jb = k * TB + b
                        if not prev and jb % HB == 0:
                            pe.wait_ge(v_ready, 1 + jb // HB)
                        last = nc.tensor.matmul(agg, v_sb[:, jb, :], ring[:, k, b, :],
                                                start=jb == 0, stop=jb == NB - 1)
                    last.then_inc(agg_tiles, 1)
                    if prev2 and k == 0:
                        pe.wait_ge(xn_ready[0], c - 1)
                        transposes(0, xt_ps)
                    if prev and k == 1:
                        pe.wait_ge(at_ready, c)
                        wait(pe, w_read, c - 1)
                        layer_product()

            aggregate(0, 0, False, False)
            aggregate(1, 1, True, False)
            with pe.Fori(1, NC // 2) as c2:
                aggregate(c2 * 2, 0, True, True)
                aggregate(c2 * 2 + 1, 1, True, True)
            pe.wait_ge(xn_ready[0], NC - 1)
            transposes(0, xt_ps)
            pe.wait_ge(at_ready, NC)
            pe.wait_ge(w_read, NC - 1)
            layer_product()
            pe.wait_ge(xn_ready[0], NC)
            transposes(0, xt_ps)

            HI, LO = 0, 1
            PAIRS = ((HI, HI), (HI, LO), (LO, HI))

            def scores(la, c, t, shifted):
                slot_free = clamped[la] if shifted else exp_done[la]
                wait(pe, slot_free, c * NS + (t - 1))
                if shifted and t == 0:
                    pe.wait_ge(shift_ready[la], c + 1)
                for u in range(SB):
                    o = s_ps[:, t % 2, ts(u, CH)]
                    for a, b in PAIRS:
                        last = nc.tensor.matmul(o, xt[la][:, a, ts(t * SB + u, P)], xt[la][:, b, ds(c * CH, CH)],
                                                start=(a, b) == (HI, HI), stop=(a, b) == PAIRS[-1] and not shifted)
                    if shifted:
                        last = nc.tensor.matmul(o, ones[0:NB, :], neg_rows[:, :, :].rearrange("b c p -> b (c p)"),
                                                start=False, stop=True)
                last.then_inc(s_done[la], 1)

            def weighted_sum(la, c, t):
                pe.wait_ge(pl_done[la], c * NS + (t + 1))
                if t == 0:
                    wait(pe, acc_out[la], c)
                for u in range(SB):
                    jb = t * SB + u
                    for b in range(CB):
                        col = ts(u * CB + b, P)
                        nc.tensor.matmul(acc_ps[:, b, 0:AW], ph_ring[:, t % LAG, col], src[la][:, jb, :],
                                         start=jb == 0, stop=False)
                        last = nc.tensor.matmul(acc_ps[:, b, F:AW], pl_ring[:, t % LAG, col],
                                                src[la][:, jb, F:AW], start=False, stop=jb == NB - 1)
                last.then_inc(pv_done[la], 1)

            def row_maxima(la):
                def block_row(b):
                    for j in range(NC):
                        wait(pe, sm_read[la], b * NC + j)
                        for n, (p, q) in enumerate(PAIRS):
                            last = nc.tensor.matmul(s_ps[:, 0, 0:CH], xt[la][:, p, ds(b * P, P)],
                                                    xt[la][:, q, ts(j, CH)], start=n == 0, stop=n == 2)
                        last.then_inc(sm_done[la], 1)

                block_row(0)
                with pe.Fori(1, NB) as b:
                    block_row(b)
                pe.wait_ge(neg_ready[la], 1)
                nc.tensor.transpose(s_ps[0:NB, 1, 0:P], ext[:, :], ident[:, :]).then_inc(neg_done[la], 1)
                pe.wait_ge(neg_ready[la], 2)

            def chunk(la, c, first, shifted):
                for t in range(NS):
                    if t >= LAG:
                        weighted_sum(la, c, t - LAG)
                    elif not first:
                        weighted_sum(la, c - 1, NS - LAG + t)
                    if la == 0 and not first and t == XT - 1:
                        pe.wait_ge(clamped[la] if shifted else exp_done[la], c * NS + t)
                        pe.wait_ge(xn_ready[1], c)
                        transposes(1, s_ps[:, (t + 1) % 2, 0:CH])
                    if la == 0 and not first and t == XT:
                        pe.wait_ge(xt_lo[1], c)
                    scores(la, c, t, shifted)
                    if first and t == LAG - 1:
                        for jb in range(NB):
                            last = nc.tensor.matmul(acc_ps[:, 0, 0:AW], ones_h[:, :], src[la][:, jb, :],
                                                    start=jb == 0, stop=jb == NB - 1)
                        last.then_inc(sums_done[la], 1)
                        pe.wait_ge(sums_out[la], 1)

            def attention(la, shifted):
                if shifted:
                    row_maxima(la)
                chunk(la, 0, True, shifted)
                with pe.Fori(1, NC) as c:
                    chunk(la, c, False, shifted)
                for t in range(LAG):
                    weighted_sum(la, NC - 1, NS - LAG + t)
                if la == 0:
                    pe.wait_ge(xn_ready[1], NC)
                    transposes(1, s_ps[:, 0, 0:CH])

            pe.wait_ge(flags, 1)
            for la in range(2):
                pe.wait_ge(xt_lo[la], NC)
                pe.wait_ge(consts_made, 7)
                with pe.If(pe.value_load(beta_big[0:1, la:la + 1]) == 0):
                    attention(la, False)
                with pe.Else():
                    attention(la, True)

        @block.scalar
        def _(act):
            for dst, s in ((w1[:, 0:F], embed), (w1[:, F:2 * F], layer[0:F, :]), (w2[:, :], layer[F:2 * F, :]),
                           (eb[:, :], embed_bias.rearrange("(a f) -> a f", a=1).to_broadcast([P, F])),
                           (lb[:, :], layer_bias.rearrange("(a f) -> a f", a=1).to_broadcast([P, F])),
                           (beta[:, 0:1], beta1.rearrange("(a f) -> a f", a=1).to_broadcast([P, 1])),
                           (beta[:, 1:2], beta2.rearrange("(a f) -> a f", a=1).to_broadcast([P, 1]))):
                act.dma_start(dst, s).then_inc(weights_in, 16)

            asks = [0, 0]

            def on(func, dst, s, **kw):
                asks[1] += 1
                act.wait_ge(asked, asks[0] + asks[1])
                nc.scalar.activation(dst, s, func, **kw).then_inc(told, 1)

            def log_terms(z, plus, minus):
                on(ACT.Ln, plus, z, bias=1.0)
                on(ACT.Ln, minus, z, bias=1.0, scale=-1.0)

            def sm(i, w):
                return small[:, i, 0:w]

            for i in range(2):
                on(ACT.Square, scr_b[:, ts(i, HB), :], scr_a[:, ts(i, HB), :])
            for i in range(2):
                on(ACT.Square, scr_b[:, ts(i, HB), :], h_sb[:, ts(i, HB), :])
            for r in range(NC):
                act.wait_ge(ht_done, r + 1)
                wait(act, gh_done, r)
                nc.scalar.activation(at_sb, ht_ps, ACT.Copy).then_inc(ht_copied, 1)
                act.wait_ge(gh_done, r + 1)
                nc.scalar.activation(h1_sb[:, ts(r, CB), :], h1_ps, ACT.Copy).then_inc(h1_copied, 1)
            for i in range(2):
                log_terms(sm(4, HB), sm(5, HB), sm(6, HB))
                on(ACT.Square, scr_b[:, ts(i, HB), :], scr_a[:, ts(i, HB), :])
                on(ACT.Tanh, sm(5, HB), sm(4, HB))
                on(ACT.Square, scr_b[:, ts(i, HB), :], scr_a[:, ts(i, HB), :])
                log_terms(sm(4, HB), sm(5, HB), sm(6, HB))
            start = asks[1]

            def split_columns(la, c, ps):
                act.wait_ge(xt_done[la], c + 1)
                nc.scalar.activation(xt[la][:, 0, ds(c * CH, CH)], ps, ACT.Copy).then_inc(xt_hi[la], 1)

            def gnn_chunk(c, parity, first):
                act.wait_ge(agg_tiles, c * NT + NT)
                if first:
                    act.wait_ge(gh_done, NC)
                else:
                    act.wait_ge(w_done, c)
                nc.scalar.activation(at_sq, acc_ps[:, parity, :], ACT.Square)
                nc.scalar.activation(at_sb, acc_ps[:, parity, :], ACT.Copy).then_inc(at_ready, 1)
                if not first:
                    split_columns(0, c - 1, xt_ps)
                on(ACT.Tanh, sm(5, CB), sm(4, CB))
                log_terms(sm(4, CB), sm(5, CB), sm(6, CB))
                on(ACT.Square, t2[:, :, :], t1[:, :, :])
                on(ACT.Tanh, sm(5, CB), sm(4, CB))
                on(ACT.Square, t2[:, :, :], t1[:, :, :])
                on(ACT.Square, t2[:, :, :], t1[:, :, :])
                on(ACT.Copy, src[0][:, ds(c * CB, CB), F:2 * F], t1[:, :, :], scale=FS)

            def turn(c, parity, first):
                asks[0], asks[1] = c * ASKS_CHUNK + start, 0
                gnn_chunk(c, parity, first)
                assert asks[1] == ASKS_CHUNK

            turn(0, 0, True)
            turn(1, 1, False)
            with act.Fori(1, NC // 2) as c2:
                turn(c2 * 2, 0, False)
                turn(c2 * 2 + 1, 1, False)
            split_columns(0, NC - 1, xt_ps)
            asks_gnn = start + NC * ASKS_CHUNK

            def exps(la, c, t, shifted):
                if shifted:
                    act.wait_ge(clamped[la], c * NS + (t + 1))
                    nc.scalar.activation(e_ring[:, t % ER, :], e_ring[:, t % ER, :], ACT.Exp,
                                         bias=p_log[:, 0:1]).then_inc(exp_done[la], 1)
                    return
                act.wait_ge(s_done[la], c * NS + (t + 1))
                wait(act, mask_done[la], c * NS + (t + 1 - ER))
                nc.scalar.activation(e_ring[:, t % ER, :], s_ps[:, t % 2, :], ACT.Exp,
                                     bias=beta_bias[:, la:la + 1], scale=beta_scale[:, la:la + 1])\
                    .then_inc(exp_done[la], 1)

            def p_hi(la, c, t):
                act.wait_ge(mask_done[la], c * NS + (t + 1))
                wait(act, pv_done[la], c * NS + (t + 1 - LAG))
                nc.scalar.activation(ph_ring[:, t % LAG, :], m_ring[:, t % LAG, :], ACT.Copy)\
                    .then_inc(ph_done[la], 1)

            def sums_leave(la, c):
                act.wait_ge(pv_done[la], c * NS + NS)
                if la == 0:
                    wait(act, xn_ready[1], c)
                else:
                    wait(act, out_ready, c)
                nc.scalar.activation(accs[:, :, :], acc_ps[:, :, 0:AW], ACT.Copy).then_inc(acc_out[la], 1)

            def next_rows(c):
                asks[0], asks[1] = c * 2 + asks_gnn, 0
                on(ACT.Square, t2[:, :, :], t1[:, :, :])
                on(ACT.Copy, src[1][:, ds(c * CB, CB), F:2 * F], t1[:, :, :], scale=FS)

            def chunk(la, c, first, shifted):
                for t in range(NS):
                    if la == 0 and not first and t == XT:
                        split_columns(1, c - 1, s_ps[:, t % 2, 0:CH])
                    exps(la, c, t, shifted)
                    if t:
                        p_hi(la, c, t - 1)
                    elif not first:
                        p_hi(la, c - 1, NS - 1)
                    if not first and t == LAG - 2:
                        sums_leave(la, c - 1)
                    if first and t == LAG - 1:
                        act.wait_ge(sums_done[la], 1)
                        nc.scalar.activation(fallback[:, :], acc_ps[:, 0, 0:AW], ACT.Copy).then_inc(sums_out[la], 1)
                    if la == 0 and not first and t == LAG + 1:
                        next_rows(c - 1)

            def attention(la, shifted):
                chunk(la, 0, True, shifted)
                with act.Fori(1, NC) as c:
                    chunk(la, c, False, shifted)
                p_hi(la, NC - 1, NS - 1)
                sums_leave(la, NC - 1)
                if la == 0:
                    next_rows(NC - 1)
                    split_columns(1, NC - 1, s_ps[:, 0, 0:CH])

            act.wait_ge(flags, 1)
            for la in range(2):
                with act.If(act.value_load(beta_big[0:1, la:la + 1]) == 0):
                    attention(la, False)
                with act.Else():
                    attention(la, True)

        @block.vector
        def _(dve):
            step = Chain(dve, vec)
            answers, asks = [0, 0], [0]
            V = nc.vector

            def ask(ins, n=1):
                ins.then_inc(asked, n)
                asks[0] += n
                dve.wait_ge(asked, answers[0] + asks[0])

            def answered(n=1):
                answers[1] += n
                dve.wait_ge(told, answers[0] + answers[1])

            def sm(i, w):
                return small[:, i, 0:w]

            def total(dst, s):
                step(V.tensor_reduce(dst, s, axis=AX.X, op=ALU.add))

            def inv_sqrt(y, v, t):
                step(V.tensor_scalar(y.bitcast(i32), v.bitcast(i32), 1, None, ALU.logical_shift_right))
                step(V.tensor_scalar(y.bitcast(i32), y.bitcast(i32), -1.0, float(0x5F3759DF), ALU.mult, ALU.add))
                for _ in range(3):
                    step(V.tensor_tensor(t, y, y, ALU.mult))
                    step(V.scalar_tensor_tensor(t, t, -0.5, v, ALU.mult, ALU.mult))
                    step(V.scalar_tensor_tensor(y, t, 1.5, y, ALU.add, ALU.mult))

            def norm(n, rn, squares, eps, w):
                v, t = sm(14, w), sm(15, w)
                step(V.tensor_scalar(v, squares, TINY, None, ALU.max))
                inv_sqrt(n, v, t)
                step(V.tensor_tensor(n, n, v, ALU.mult))
                step(V.tensor_scalar(n, n, eps, None, ALU.max))
                step(V.reciprocal(rn, n))

            def atanh_over(c, n, rn, w):
                z, lp, lm, u, s = (sm(i, w) for i in (4, 5, 6, 7, 8))
                ask(V.tensor_scalar(z, n, MAX_TANH, None, ALU.min), 2)
                step(V.tensor_tensor(u, z, z, ALU.mult))
                step(V.tensor_scalar(s, u, 1.0 / 13, None, ALU.mult))
                for k in (11, 9, 7, 5, 3):
                    step(V.scalar_tensor_tensor(s, s, 1.0 / k, u, ALU.add, ALU.mult))
                step(V.scalar_tensor_tensor(s, s, 1.0, z, ALU.add, ALU.mult))
                answered(2)
                step(V.tensor_tensor(lp, lp, lm, ALU.subtract))
                step(V.scalar_tensor_tensor(s, lp, -0.5, s, ALU.mult, ALU.add))
                step(V.tensor_scalar(u, z, SERIES, None, ALU.is_lt))
                step(V.tensor_tensor(s, s, u, ALU.mult))
                step(V.scalar_tensor_tensor(s, lp, 0.5, s, ALU.mult, ALU.add))
                step(V.tensor_tensor(c, s, rn, ALU.mult))

            def gnn_product(dst, w_in, scr, c, bias, y, w):
                gb, ww, al, xy, x2 = (sm(i, w) for i in (9, 10, 11, 12, 13))
                answered()
                total(ww, scr)
                step(V.tensor_tensor(scr, w_in, over_b(bias, w), ALU.mult))
                total(gb, scr)
                z, th = sm(4, w), sm(5, w)
                norm(z, th, ww, 0.0, w)
                step(V.tensor_tensor(z, z, c, ALU.mult))
                ask(V.tensor_scalar(z, z, EPS, None, ALU.max))
                step(V.reciprocal(al, z))
                step(V.tensor_tensor(al, al, c, ALU.mult))
                answered()
                step(V.tensor_tensor(al, al, th, ALU.mult))
                step(V.tensor_tensor(xy, al, gb, ALU.mult))
                step(V.tensor_tensor(x2, al, al, ALU.mult))
                step(V.tensor_tensor(x2, x2, ww, ALU.mult))
                step(V.tensor_scalar(xy, xy, 2.0, 1.0, ALU.mult, ALU.add))
                step(V.scalar_tensor_tensor(gb, x2, y, xy, ALU.mult, ALU.add))
                step(V.tensor_scalar(gb, gb, EPS, None, ALU.max))
                step(V.reciprocal(gb, gb))
                step(V.scalar_tensor_tensor(xy, xy, y, al, ALU.add, ALU.mult))
                step(V.tensor_tensor(xy, xy, gb, ALU.mult))
                step(V.tensor_scalar(x2, x2, -1.0, 1.0, ALU.mult, ALU.add))
                step(V.tensor_tensor(x2, x2, gb, ALU.mult))
                step(V.tensor_tensor(scr, over_b(bias, w), over_f(x2), ALU.mult))
                step(V.tensor_tensor(dst, w_in, over_f(xy), ALU.mult))
                step(V.tensor_tensor(dst, dst, scr, ALU.add))

            dve.wait_ge(weights_in, 16 * 7)
            for i, b in enumerate((eb, lb)):
                step(V.tensor_tensor(bsq[:, :], b[:, :], b[:, :], ALU.mult))
                total(y2[:, i:i + 1], bsq[:, :])
            step(V.tensor_scalar(beta_nsign[:, :], beta[:, :], -1.0, None, ALU.mult))
            step(V.tensor_tensor(beta_abs[:, :], beta[:, :], beta_nsign[:, :], ALU.max))
            step(V.tensor_scalar(beta_scale[:, :], beta[:, :], 1.0 / FS ** 2, None, ALU.mult))
            step(V.tensor_scalar(beta_bias[:, :], beta_abs[:, :], -1.0, P_LOG, ALU.mult, ALU.add))
            step(V.tensor_scalar(beta_sign[:, :], beta[:, :], 0.0, None, ALU.is_ge))
            step(V.tensor_scalar(beta_sign[:, :], beta_sign[:, :], 2.0, -1.0, ALU.mult, ALU.add))
            step(V.tensor_scalar(beta_nsign[:, :], beta_sign[:, :], -1.0, None, ALU.mult))
            V.tensor_scalar(beta_big[:, :], beta_abs[:, :], BETA_MAX, None, ALU.is_gt).then_inc(flags, 1)

            half = [ts(i, HB) for i in range(2)]
            for i in range(2):
                dve.wait_ge(x_in[i], 16)
                total(sm(i, HB), x_sb[:, half[i], :])
                step(V.tensor_scalar(sm(i, HB), sm(i, HB), 1.0 / F, None, ALU.mult))
                ask(V.tensor_tensor(scr_a[:, half[i], :], x_sb[:, half[i], :], over_f(sm(i, HB)), ALU.subtract))
            for i in range(2):
                answered()
                total(sm(i, HB), scr_b[:, half[i], :])
                step(V.tensor_scalar(sm(i, HB), sm(i, HB), 1.0 / F, LN_EPS, ALU.mult, ALU.add))
                inv_sqrt(sm(2, HB), sm(i, HB), sm(3, HB))
                ask(V.scalar_tensor_tensor(h_sb[:, half[i], :], scr_a[:, half[i], :], 0.0, over_f(sm(2, HB)),
                                           ALU.max, ALU.mult))
                V.tensor_copy(sm(3, HB), sm(2, HB)).then_inc(h_ready, 1)
            for i in range(2):
                answered()
                total(hh[:, half[i]], scr_b[:, half[i], :])
            for r in range(NC):
                dve.wait_ge(gh_done, r + 1)
                V.tensor_copy(scr_a[:, ts(r, CB), :], g_ps).then_inc(g_copied, 1)
            dve.wait_ge(g_copied, NC)
            for i in range(2):
                g = scr_a[:, half[i], :]
                norm(sm(0, HB), sm(1, HB), hh[:, half[i]], EPS, HB)
                atanh_over(sm(2, HB), sm(0, HB), sm(1, HB), HB)
                ask(V.tensor_copy(sm(3, HB), sm(2, HB)))
                gnn_product(g, g, scr_b[:, half[i], :], sm(3, HB), eb[:, :], y2[:, 0:1], HB)
                ask(V.tensor_copy(sm(3, HB), sm(2, HB)))
                answered()
                total(sm(3, HB), scr_b[:, half[i], :])
                norm(sm(0, HB), sm(1, HB), sm(3, HB), EPS, HB)
                atanh_over(sm(2, HB), sm(0, HB), sm(1, HB), HB)
                V.tensor_tensor(v_sb[:, half[i], :], g, over_f(sm(2, HB)), ALU.mult).then_inc(v_ready, 1)
            assert asks[0] == answers[1]
            start = answers[1]
            steps_start = step.n

            def split_columns(la, c, ps):
                dve.wait_ge(xt_hi[la], c + 1)
                V.tensor_tensor(xt[la][:, 1, ds(c * CH, CH)], ps, xt[la][:, 0, ds(c * CH, CH)], ALU.subtract)\
                    .then_inc(xt_lo[la], 1)

            def attention_rows(la, c, rows):
                answered(2)
                V.scalar_tensor_tensor(src[la][:, rows, 0:F], t1[:, :, :], FS, src[la][:, rows, F:2 * F],
                                       ALU.mult, ALU.subtract)
                total(sm(2, CB), t2[:, :, :])
                norm(sm(0, CB), sm(1, CB), sm(2, CB), NORM_EPS, CB)
                step(V.tensor_scalar(sm(1, CB), sm(1, CB), FS, None, ALU.mult))
                V.tensor_tensor(t3[:, :, :], t1[:, :, :], over_f(sm(1, CB)), ALU.mult).then_inc(xn_ready[la], 1)

            def gnn_chunk(c):
                rows = ds(c * CB, CB)
                dve.wait_ge(w_done, c + 1)
                norm(sm(4, CB), sm(1, CB), n_ps, EPS, CB)
                ask(V.tensor_copy(sm(2, CB), sm(4, CB)))
                answered()
                step(V.tensor_tensor(sm(3, CB), sm(5, CB), sm(1, CB), ALU.mult))
                step(V.tensor_tensor(sm(2, CB), sm(3, CB), sm(3, CB), ALU.mult))
                step(V.tensor_tensor(sm(2, CB), sm(2, CB), n_ps, ALU.mult))
                step(V.tensor_tensor(sm(2, CB), sm(2, CB), hh[:, rows], ALU.add))
                norm(sm(0, CB), sm(1, CB), sm(2, CB), EPS, CB)
                atanh_over(sm(2, CB), sm(0, CB), sm(1, CB), CB)
                step(V.tensor_tensor(t1[:, :, :], w_ps, over_f(sm(3, CB)), ALU.mult))
                V.tensor_copy(sm(0, CB), sm(3, CB)).then_inc(w_read, 1)
                ask(V.tensor_tensor(t1[:, :, :], t1[:, :, :], h1_sb[:, rows, :], ALU.add))
                gnn_product(t1[:, :, :], t1[:, :, :], t2[:, :, :], sm(2, CB), lb[:, :], y2[:, 1:2], CB)
                step(V.tensor_tensor(x_sb[:, rows, :], x_sb[:, rows, :], t1[:, :, :], ALU.add))
                V.memset(sm(1, CB), 0.0)
                total(sm(0, CB), x_sb[:, rows, :])
                step(V.tensor_scalar(sm(0, CB), sm(0, CB), 1.0 / F, None, ALU.mult))
                ask(V.tensor_tensor(t1[:, :, :], x_sb[:, rows, :], over_f(sm(0, CB)), ALU.subtract))
                answered()
                total(sm(0, CB), t2[:, :, :])
                step(V.tensor_scalar(sm(0, CB), sm(0, CB), 1.0 / F, LN_EPS, ALU.mult, ALU.add))
                inv_sqrt(sm(1, CB), sm(0, CB), sm(3, CB))
                ask(V.scalar_tensor_tensor(t1[:, :, :], t1[:, :, :], 0.0, over_f(sm(1, CB)), ALU.max, ALU.mult), 2)
                attention_rows(0, c, rows)
                split_columns(0, c, xt_ps)

            STEPS = 118

            def gnn_turn(c):
                step.base, step.n = c * STEPS + steps_start, 0
                answers[0], answers[1], asks[0] = c * ASKS_CHUNK + start, 0, 0
                gnn_chunk(c)
                assert step.n == STEPS and answers[1] == ASKS_CHUNK, (step.n, answers[1])

            gnn_turn(0)
            with dve.Fori(1, NC) as c:
                gnn_turn(c)
            steps_gnn = steps_start + NC * STEPS
            asks_gnn = start + NC * ASKS_CHUNK

            tile_base = [16 * NC * (1 + la) for la in range(2)]

            def clamp(la, c, t):
                dve.wait_ge(s_done[la], c * NS + (t + 1))
                wait(dve, mask_done[la], c * NS + (t + 1 - ER))
                V.tensor_scalar(e_ring[:, t % ER, :], s_ps[:, t % 2, :], beta_scale[:, la:la + 1], 0.0,
                                ALU.mult, ALU.min).then_inc(clamped[la], 1)

            def mask(la, c, t):
                k, half_tile = t * SB // TB, t * SB % TB
                dve.wait_ge(exp_done[la], c * NS + (t + 1))
                if half_tile == 0:
                    dve.wait_ge(tile_in[k], 16 * c + (tile_base[la] + 16))
                wait(dve, pl_done[la], c * NS + (t + 1 - LAG))
                V.scalar_tensor_tensor(m_ring[:, t % LAG, :], ring[:, k, half_tile:half_tile + SB, :]
                                       .rearrange("p b i -> p (b i)"), 0.0, e_ring[:, t % ER, :],
                                       ALU.is_gt, ALU.mult).then_inc(mask_done[la], 1)

            def p_lo(la, c, t):
                dve.wait_ge(ph_done[la], c * NS + (t + 1))
                wait(dve, pv_done[la], c * NS + (t + 1 - LAG))
                V.tensor_tensor(pl_ring[:, t % LAG, :], m_ring[:, t % LAG, :], ph_ring[:, t % LAG, :],
                                ALU.subtract).then_inc(pl_done[la], 1)

            def new_rows(la, c):
                rows = ds(c * CB, CB)
                dve.wait_ge(acc_out[la], c + 1)
                den = accs[:, :, 2 * F]
                step(V.tensor_scalar(zero[:, :], den, 0.0, None, ALU.is_equal))
                for b in range(CB):
                    ins = V.scalar_tensor_tensor(accs[:, b, :], fallback[:, :], zero[:, b:b + 1], accs[:, b, :],
                                                 ALU.mult, ALU.add)
                step(ins)
                step(V.reciprocal(sm(0, CB), den))
                step(V.tensor_tensor(t2[:, :, :], accs[:, :, 0:F], accs[:, :, F:2 * F], ALU.add))
                step(V.tensor_tensor(t2[:, :, :], t2[:, :, :], over_f(sm(0, CB)), ALU.mult))
                leaky = V.scalar_tensor_tensor(t1[:, :, :], t2[:, :, :], LEAK, t2[:, :, :], ALU.mult, ALU.max)
                if la == 0:
                    ask(leaky, 2)
                else:
                    step(leaky)
                    V.tensor_tensor(x_sb[:, rows, :], x_sb[:, rows, :], t1[:, :, :], ALU.add).then_inc(out_ready, 1)

            ROWS0, ROWS1 = 22, 6

            def turn0(c):
                step.base, step.n = c * ROWS0 + steps_gnn, 0
                answers[0], answers[1], asks[0] = c * 2 + asks_gnn, 0, 0
                new_rows(0, c)
                return ds(c * CB, CB)

            def chunk(la, c, first, shifted):
                for t in range(NS):
                    if shifted:
                        if t == 0 and not first:
                            shift_rows(la, c)
                        clamp(la, c, t)
                    mask(la, c, t)
                    if t:
                        p_lo(la, c, t - 1)
                    elif not first:
                        p_lo(la, c - 1, NS - 1)
                    if first:
                        continue
                    if t == LAG:
                        if la == 0:
                            turn0(c - 1)
                        else:
                            step.base, step.n = (c - 1) * ROWS1 + steps_la0, 0
                            new_rows(1, c - 1)
                            assert step.n == ROWS1, step.n
                    if la == 0 and t == LAG + 1:
                        attention_rows(1, c - 1, ds((c - 1) * CB, CB))
                        assert step.n == ROWS0, step.n
                    if la == 0 and t == XT - 1:
                        split_columns(1, c - 1, s_ps[:, (t + 1) % 2, 0:CH])

            steps_la0 = steps_gnn + NC * ROWS0

            def shift_rows(la, c):
                wait(dve, s_done[la], c * NS)
                V.tensor_tensor(neg_rows[:, :, :], neg_t[:, :].unsqueeze(1).to_broadcast([NB, CB, P]),
                                ident[0:NB, ds(c * CB, CB)].unsqueeze(2).to_broadcast([NB, CB, P]),
                                ALU.mult).then_inc(shift_ready[la], 1)

            def row_maxima(la):
                with dve.Fori(0, NB) as b:
                    dve.wait_ge(rows_in[la], b * 16 + 16)
                    for j in range(NC):
                        V.tensor_scalar(t1[:, :, :].rearrange("p b f -> p (b f)"), adj_rows[:, ts(j, CH)],
                                        0.0, -1e9, ALU.is_le, ALU.mult).then_inc(max_step[la], 1)
                        dve.wait_ge(max_step[la], b * (2 * NC) + (2 * j + 1))
                        dve.wait_ge(sm_done[la], b * NC + (j + 1))
                        V.scalar_tensor_tensor(t2[:, :, :].rearrange("p b f -> p (b f)"), s_ps[:, 0, 0:CH],
                                               beta_sign[:, la:la + 1], t1[:, :, :].rearrange("p b f -> p (b f)"),
                                               ALU.mult, ALU.add).then_inc(max_step[la], 1)
                        dve.wait_ge(max_step[la], b * (2 * NC) + (2 * j + 2))
                        V.tensor_reduce(ext8[:, j:j + 1], t2[:, :, :].rearrange("p b f -> p (b f)"),
                                        axis=AX.X, op=ALU.max).then_inc(sm_read[la], 1)
                    dve.wait_ge(sm_read[la], b * NC + NC)
                    V.tensor_reduce(ext[:, ds(b, 1)], ext8[:, :], axis=AX.X, op=ALU.max).then_inc(rows_used[la], 1)
                dve.wait_ge(rows_used[la], NB)
                V.tensor_scalar(ext[:, :], ext[:, :], -2.0 * FS ** 2, beta_nsign[:, la:la + 1],
                                ALU.max, ALU.mult).then_inc(neg_ready[la], 1)
                dve.wait_ge(neg_done[la], 1)
                V.tensor_copy(neg_t[:, :], s_ps[0:NB, 1, 0:P]).then_inc(neg_ready[la], 1)
                dve.wait_ge(neg_ready[la], 2)

            def attention(la, shifted):
                if shifted:
                    row_maxima(la)
                    shift_rows(la, 0)
                chunk(la, 0, True, shifted)
                with dve.Fori(1, NC) as c:
                    chunk(la, c, False, shifted)
                p_lo(la, NC - 1, NS - 1)
                if la == 0:
                    turn0(NC - 1)
                    attention_rows(1, NC - 1, ds((NC - 1) * CB, CB))
                    split_columns(1, NC - 1, s_ps[:, 0, 0:CH])
                else:
                    step.base, step.n = (NC - 1) * ROWS1 + steps_la0, 0
                    new_rows(1, NC - 1)

            dve.wait_ge(flags, 1)
            for la in range(2):
                with dve.If(dve.value_load(beta_big[0:1, la:la + 1]) == 0):
                    attention(la, False)
                with dve.Else():
                    attention(la, True)


def kernel(x, adj, L0_gnn_embed, L0_gnn_layer, L0_gnn_embed_bias, L0_gnn_layer_bias, L1_gnn_beta1, L1_gnn_beta2):
    import concourse.bacc as bacc
    from concourse.bass_utils import run_bass_kernel_spmd

    arrays = {"x": x, "adj": adj, "adj_t": np.asarray(adj).T, "embed": L0_gnn_embed, "layer": L0_gnn_layer,
              "embed_bias": L0_gnn_embed_bias, "layer_bias": L0_gnn_layer_bias,
              "beta1": L1_gnn_beta1, "beta2": L1_gnn_beta2}
    arrays = {f"in_{k}": np.ascontiguousarray(a) for k, a in arrays.items()}
    nc = bacc.Bacc("TRN2", target_bir_lowering=False, num_devices=1)
    args = [nc.dram_tensor(k, a.shape, mybir.dt.float32, kind="ExternalInput").ap() for k, a in arrays.items()]
    out = nc.dram_tensor("out_0", arrays["in_x"].shape, mybir.dt.float32, kind="ExternalOutput").ap()
    build(nc, *args, out)
    return run_bass_kernel_spmd(nc, [arrays], core_ids=[0]).results[0]["out_0"]
```

```python
import numpy as np
import concourse.bass as bass
import concourse.mybir as mybir
from contextlib import ExitStack


def build(nc, x, adj, adj_t, embed, layer, embed_bias, layer_bias, beta1, beta2, out):
    f32, f16, i32 = mybir.dt.float32, mybir.dt.float16, mybir.dt.int32
    ACT, ALU, AX = mybir.ActivationFunctionType, mybir.AluOpType, mybir.AxisListType
    ts, ds = bass.ts, bass.ds

    N, F = x.shape
    P = 128
    NB = N // P
    CH = 512
    CB = CH // P
    NC = N // CH
    TB = 4
    NT = NB // TB
    SB = 2
    NS = NB // SB
    ER = 2
    LAG = 4
    AW = 2 * F + 1
    XP = 4
    EPS, MAX_TANH, LN_EPS, NORM_EPS, LEAK = 1e-7, 1.0 - 1e-6, 1e-5, 1e-12, 0.3
    TINY = 1e-30
    FS = 256.0
    P_LOG = 15 * float(np.log(2.0))
    BETA_MAX = 4.0
    SERIES = 0.25

    ctx = ExitStack()
    with ctx:
        def sb(name, shape, dt=f32):
            return ctx.enter_context(nc.sbuf_tensor(name, shape, dt))

        def sem(name):
            return ctx.enter_context(nc.semaphore(name))

        ring = sb("ring", [P, NT, TB, CH])
        x_sb = sb("x_sb", [P, NB, F])
        h_all = sb("h_all", [P, max(NB * F, LAG * SB * CH)])
        h_sb = h_all[:, 0:NB * F].rearrange("p (b f) -> p b f", f=F)
        p_rings = h_all[:, 0:LAG * SB * CH].bitcast(f16).rearrange("p (s r n) -> p s r n", s=2, r=LAG)
        ph_ring, pl_ring = p_rings[:, 0], p_rings[:, 1]
        set1 = sb("set1", [P, 2 * NB * F + NB])
        v_sb = set1[:, 0:NB * F].rearrange("p (b f) -> p b f", f=F)
        h1_sb = set1[:, NB * F:2 * NB * F].rearrange("p (b f) -> p b f", f=F)
        set1_h = set1[:, :].bitcast(f16)
        src0_all = sb("src0", [P, NB * AW], f16)
        src0 = src0_all[:, :].rearrange("p (b w) -> p b w", w=AW)
        xt0 = sb("xt0", [F, 2, N], f16)
        src = [src0, set1_h[:, 2 * N:2 * N + NB * AW].rearrange("p (b w) -> p b w", w=AW)]
        xt = [xt0, set1_h[:, 0:2 * N].rearrange("p (s n) -> p s n", s=2)]

        work = sb("work", [P, (ER + LAG) * SB * CH])
        e_ring = work[:, 0:ER * SB * CH].rearrange("p (r n) -> p r n", r=ER)
        m_ring = work[:, ER * SB * CH:(ER + LAG) * SB * CH].rearrange("p (r n) -> p r n", r=LAG)
        adj_rows = work[:, 0:N]
        scr_a = work[:, 0:NB * F].rearrange("p (b f) -> p b f", f=F)
        scr_b = xt0[:, :, :].rearrange("p s n -> p (s n)").bitcast(f32)[:, 0:NB * F].rearrange("p (b f) -> p b f", f=F)
        accs = sb("accs", [P, CB, AW])
        fallback = sb("fallback", [P, AW])
        mean_row = sb("mean_row", [P, F])
        t1 = sb("t1", [P, CB, F])
        t2 = sb("t2", [P, CB, F])
        t3 = sb("t3", [P, CB, F])
        at_sb = accs[:, :, :].rearrange("p b w -> p (b w)")[:, 0:CH]
        at_sq = accs[:, :, :].rearrange("p b w -> p (b w)")[:, CH:2 * CH]

        w1 = sb("w1", [F, 2 * F])
        w2 = sb("w2", [F, F])
        eb = sb("eb", [P, F])
        lb = sb("lb", [P, F])
        bsq = sb("bsq", [P, F])
        y2 = sb("y2", [P, 2])
        beta = sb("beta", [P, 2])
        beta_abs = sb("beta_abs", [P, 2])
        beta_big = sb("beta_big", [P, 2], i32)
        beta_scale = sb("beta_scale", [P, 2])
        beta_bias = sb("beta_bias", [P, 2])
        beta_sign = sb("beta_sign", [P, 2])
        beta_nsign = sb("beta_nsign", [P, 2])
        p_log = sb("p_log", [P, 1])
        ident = sb("ident", [P, P])
        ones = sb("ones", [P, P])
        ht_sb = src0_all[:, 0:2 * N].bitcast(f32)
        web = sb("web", [F, 1])
        ones_h = sb("ones_h", [P, P], f16)
        small = sb("small", [P, 16, NB])
        hh = sb("hh", [P, NB])
        zero = sb("zero", [P, CB])
        neg_t = sb("neg_t", [NB, P])
        neg_rows = sb("neg_rows", [NB, CB, P])
        stats = sb("stats", [P, NB, 6])
        mean_var = sb("mean_var", [P, NB, 2])
        ext = sb("ext", [P, NB])
        ext8 = sb("ext8", [P, NC])

        s_ps = ctx.enter_context(nc.psum_tensor("s_ps", [P, 2, SB * CH], f32))
        acc_ps = ctx.enter_context(nc.psum_tensor("acc_ps", [P, CB, 512], f32))
        g_ps = [s_ps[:, i, 0:CH].rearrange("p (b f) -> p b f", f=F) for i in range(2)]
        h1_ps = [s_ps[:, i // 2, ts(i % 2, CH)].rearrange("p (b f) -> p b f", f=F) for i in range(4)]
        gb_ps = acc_ps[:, 0, 0:NB]
        w_ps = s_ps[:, 0, 0:CH].rearrange("p (b f) -> p b f", f=F)
        xt_ps = s_ps[:, 1, 0:CH]
        ht_ps = [acc_ps[:, 2 + i, :] for i in range(2)]
        n_ps = acc_ps[:, 2, 0:CB]

        x_in = [sem(f"x_in{i}") for i in range(XP)]
        embed_in = sem("embed_in")
        weights_in = sem("weights_in")
        consts_made = sem("consts_made")
        tile_in = [sem(f"tile_in{k}") for k in range(NT)]
        agg_tiles = sem("agg_tiles")
        vec = sem("vec")
        asked = sem("asked")
        told = sem("told")
        flags = sem("flags")
        mean_made = sem("mean_made")
        xs_ready = sem("xs_ready")
        h_ready = sem("h_ready")
        web_made = sem("web_made")
        ht_done = sem("ht_done")
        ht_copied = sem("ht_copied")
        g_done = sem("g_done")
        gb_done = sem("gb_done")
        h1_done = sem("h1_done")
        g_copied = sem("g_copied")
        h1_copied = sem("h1_copied")
        v_ready = sem("v_ready")
        bias_part = sem("bias_part")
        at_ready = sem("at_ready")
        w_done = sem("w_done")
        w_read = sem("w_read")
        xn_ready = [sem(f"xn_ready{i}") for i in range(2)]
        xt_done = [sem(f"xt_done{i}") for i in range(2)]
        xt_hi = [sem(f"xt_hi{i}") for i in range(2)]
        xt_lo = [sem(f"xt_lo{i}") for i in range(2)]
        s_done = [sem(f"s_done{i}") for i in range(2)]
        exp_done = [sem(f"exp_done{i}") for i in range(2)]
        mask_done = [sem(f"mask_done{i}") for i in range(2)]
        ph_done = [sem(f"ph_done{i}") for i in range(2)]
        pl_done = [sem(f"pl_done{i}") for i in range(2)]
        pv_done = [sem(f"pv_done{i}") for i in range(2)]
        acc_out = [sem(f"acc_out{i}") for i in range(2)]
        sums_done = [sem(f"sums_done{i}") for i in range(2)]
        sums_out = [sem(f"sums_out{i}") for i in range(2)]
        clamped = [sem(f"clamped{i}") for i in range(2)]
        rows_in = [sem(f"rows_in{i}") for i in range(2)]
        rows_used = [sem(f"rows_used{i}") for i in range(2)]
        sm_done = [sem(f"sm_done{i}") for i in range(2)]
        sm_read = [sem(f"sm_read{i}") for i in range(2)]
        neg_done = [sem(f"neg_done{i}") for i in range(2)]
        neg_ready = [sem(f"neg_ready{i}") for i in range(2)]
        shift_ready = [sem(f"shift_ready{i}") for i in range(2)]
        max_step = [sem(f"max_step{i}") for i in range(2)]
        out_ready = sem("out_ready")
        stored = sem("stored")

        adj_tiles = adj_t.rearrange("(t b p) i -> t p b i", b=TB, p=P)
        x_v = x.rearrange("(b p) f -> p b f", p=P)
        out_v = out.rearrange("(b p) f -> p b f", p=P)
        adj_v = adj.rearrange("(b p) j -> b p j", p=P)

        def wait(eng, s, value):
            if not isinstance(value, int) or value > 0:
                eng.wait_ge(s, value)

        class Chain:
            def __init__(self, eng, s):
                self.eng, self.s, self.base, self.n = eng, s, 0, 0

            def __call__(self, ins):
                ins.then_inc(self.s, 1)
                self.n += 1
                self.eng.wait_ge(self.s, self.base + self.n)

        def over_f(ap):
            return ap.unsqueeze(2).to_broadcast([P, ap.shape[1], F])

        def over_b(ap, b):
            return ap.unsqueeze(1).to_broadcast([P, b, F])

        ASKS_CHUNK = 6
        ASKS_ROWS = (3, 1)
        block = ctx.enter_context(nc.Block())

        @block.sync
        def _(sp):
            for i in range(XP):
                sp.dma_start(x_sb[:, ts(i, NB // XP), :], x_v[:, ts(i, NB // XP), :]).then_inc(x_in[i], 16)

            def load(k, c):
                sp.dma_start(ring[:, k, :, :], adj_tiles[k, :, :, ds(c * CH, CH)]).then_inc(tile_in[k], 16)

            for k in range(NT):
                load(k, 0)
            with sp.Fori(1, NC) as c:
                for k in range(NT):
                    sp.wait_ge(agg_tiles, (c - 1) * NT + (k + 1))
                    load(k, c)
            for la in range(2):
                for k in range(NT):
                    if la == 0:
                        sp.wait_ge(agg_tiles, (NC - 1) * NT + (k + 1))
                    else:
                        sp.wait_ge(mask_done[0], (NC - 1) * NS + 2 * k + 2)
                    load(k, 0)
                with sp.Fori(1, NC) as c:
                    for k in range(NT):
                        sp.wait_ge(mask_done[la], (c - 1) * NS + (2 * k + 2))
                        load(k, c)

        @block.gpsimd
        def _(pool):
            pool.memset(ident[:, :], 0.0).then_inc(consts_made, 1)
            pool.memset(ones[:, :], 1.0).then_inc(consts_made, 1)
            pool.memset(ones_h[:, :], 1.0).then_inc(consts_made, 1)
            pool.memset(p_log[:, :], P_LOG).then_inc(consts_made, 1)
            pool.wait_ge(consts_made, 4)
            pool.affine_select(out=ident[:, :], in_=ident[:, :], compare_op=ALU.not_equal, fill=1.0,
                               base=0, pattern=[[-1, P]], channel_multiplier=1).then_inc(consts_made, 1)
            pool.wait_ge(h1_done, NC)
            pool.memset(src[0][:, :, 2 * F:AW], FS).then_inc(consts_made, 1)
            pool.wait_ge(xn_ready[0], NC)
            pool.wait_ge(agg_tiles, NC * NT)
            pool.memset(src[1][:, :, 2 * F:AW], FS).then_inc(consts_made, 1)
            pool.wait_ge(flags, 1)
            for la in range(2):
                with pool.If(pool.value_load(beta_big[0:1, la:la + 1]) != 0):
                    if la == 0:
                        pool.wait_ge(xt_lo[0], NC)
                    else:
                        pool.wait_ge(pl_done[0], NC * NS)
                        pool.wait_ge(ph_done[0], NC * NS)
                    pool.dma_start(adj_rows, adj_v[0, :, :]).then_inc(rows_in[la], 16)
                    with pool.Fori(1, NB) as b:
                        pool.wait_ge(rows_used[la], b)
                        pool.dma_start(adj_rows, adj_v[ds(b, 1), :, :].rearrange("o p j -> p (o j)"))\
                            .then_inc(rows_in[la], 16)
            with pool.Fori(0, NC) as c:
                pool.wait_ge(out_ready, c + 1)
                pool.dma_start(out_v[:, ds(c * CB, CB), :], x_sb[:, ds(c * CB, CB), :]).then_inc(stored, 16)
            pool.wait_ge(stored, 16 * NC)

        @block.tensor
        def _(pe):
            pe.wait_ge(consts_made, 5)
            pe.wait_ge(embed_in, 16 * 2)

            def h_transposes(r):
                pe.wait_ge(h_ready, r + 1)
                wait(pe, ht_copied, r - 1)
                for b in range(CB):
                    last = nc.tensor.transpose(ht_ps[r % 2][:, ts(b, P)], h_sb[:, r * CB + b, :], ident[:, :])
                last.then_inc(ht_done, 1)

            h_transposes(0)
            for r in range(NC):
                if r + 1 < NC:
                    h_transposes(r + 1)
                pe.wait_ge(ht_copied, r + 1)
                wait(pe, g_copied, r - 1)
                for b in range(CB):
                    last = nc.tensor.matmul(g_ps[r % 2][:, b, :], ht_sb[:, ts(r * CB + b, P)], w1[:, 0:F],
                                            start=True, stop=True)
                last.then_inc(g_done, 1)
            pe.wait_ge(web_made, 1)
            for b in range(NB):
                last = nc.tensor.matmul(gb_ps[:, b:b + 1], ht_sb[:, ts(b, P)], web[:, :], start=True, stop=True)
            last.then_inc(gb_done, 1)
            pe.wait_ge(weights_in, 16 * 5)
            pe.wait_ge(g_copied, NC)
            for r in range(NC):
                wait(pe, h1_copied, r - 3)
                for b in range(CB):
                    last = nc.tensor.matmul(h1_ps[r % 4][:, b, :], ht_sb[:, ts(r * CB + b, P)], w1[:, F:2 * F],
                                            start=True, stop=True)
                last.then_inc(h1_done, 1)

            def layer_product():
                for b in range(CB):
                    nc.tensor.matmul(w_ps[:, b, :], at_sb[:, ts(b, P)], w2[:, :], start=True, stop=True)
                for b in range(CB):
                    last = nc.tensor.matmul(n_ps[:, b:b + 1], at_sq[:, ts(b, P)], ones[:, 0:1],
                                            start=True, stop=True)
                last.then_inc(w_done, 1)

            def transposes(la, out_ps):
                for b in range(CB):
                    last = nc.tensor.transpose(out_ps[:, ts(b, P)], t3[:, b, :], ident[:, :])
                last.then_inc(xt_done[la], 1)

            def aggregate(c, parity, prev, prev2):
                agg = acc_ps[:, parity, :]
                for k in range(NT):
                    pe.wait_ge(tile_in[k], 16 * c + 16)
                    if prev2 and k == 0:
                        pe.wait_ge(at_ready, c - 1)
                    for b in range(TB):
                        jb = k * TB + b
                        if not prev:
                            pe.wait_ge(v_ready, jb + 1)
                        last = nc.tensor.matmul(agg, v_sb[:, jb, :], ring[:, k, b, :],
                                                start=jb == 0, stop=jb == NB - 1)
                    last.then_inc(agg_tiles, 1)
                    if prev and k == 0:
                        pe.wait_ge(at_ready, c)
                        wait(pe, w_read, c - 1)
                        layer_product()
                    if prev2 and k == 3:
                        pe.wait_ge(xn_ready[0], c - 1)
                        transposes(0, xt_ps)

            aggregate(0, 0, False, False)
            aggregate(1, 1, True, False)
            with pe.Fori(1, NC // 2) as c2:
                aggregate(c2 * 2, 0, True, True)
                aggregate(c2 * 2 + 1, 1, True, True)
            pe.wait_ge(at_ready, NC)
            pe.wait_ge(w_read, NC - 1)
            layer_product()
            pe.wait_ge(xn_ready[0], NC - 1)
            transposes(0, xt_ps)
            pe.wait_ge(xn_ready[0], NC)
            transposes(0, xt_ps)

            HI, LO = 0, 1
            PAIRS = ((HI, HI), (HI, LO), (LO, HI))

            def scores(la, c, t, shifted):
                slot_free = clamped[la] if shifted else exp_done[la]
                wait(pe, slot_free, c * NS + (t - 1))
                if shifted and t == 0:
                    pe.wait_ge(shift_ready[la], c + 1)
                for u in range(SB):
                    o = s_ps[:, t % 2, ts(u, CH)]
                    for a, b in PAIRS:
                        last = nc.tensor.matmul(o, xt[la][:, a, ts(t * SB + u, P)], xt[la][:, b, ds(c * CH, CH)],
                                                start=(a, b) == (HI, HI), stop=(a, b) == PAIRS[-1] and not shifted)
                    if shifted:
                        last = nc.tensor.matmul(o, ones[0:NB, :], neg_rows[:, :, :].rearrange("b c p -> b (c p)"),
                                                start=False, stop=True)
                last.then_inc(s_done[la], 1)

            def weighted_sum(la, c, t):
                pe.wait_ge(pl_done[la], c * NS + (t + 1))
                if t == 0:
                    wait(pe, acc_out[la], c)
                for u in range(SB):
                    jb = t * SB + u
                    for b in range(CB):
                        col = ts(u * CB + b, P)
                        nc.tensor.matmul(acc_ps[:, b, 0:AW], ph_ring[:, t % LAG, col], src[la][:, jb, :],
                                         start=jb == 0, stop=False)
                        last = nc.tensor.matmul(acc_ps[:, b, F:AW], pl_ring[:, t % LAG, col],
                                                src[la][:, jb, F:AW], start=False, stop=jb == NB - 1)
                last.then_inc(pv_done[la], 1)

            def row_maxima(la):
                def block_row(b):
                    for j in range(NC):
                        wait(pe, sm_read[la], b * NC + j)
                        for n, (p, q) in enumerate(PAIRS):
                            last = nc.tensor.matmul(s_ps[:, 0, 0:CH], xt[la][:, p, ds(b * P, P)],
                                                    xt[la][:, q, ts(j, CH)], start=n == 0, stop=n == 2)
                        last.then_inc(sm_done[la], 1)

                block_row(0)
                with pe.Fori(1, NB) as b:
                    block_row(b)
                pe.wait_ge(neg_ready[la], 1)
                nc.tensor.transpose(s_ps[0:NB, 1, 0:P], ext[:, :], ident[:, :]).then_inc(neg_done[la], 1)
                pe.wait_ge(neg_ready[la], 2)

            def chunk(la, c, first, shifted):
                for t in range(NS):
                    if t >= LAG:
                        weighted_sum(la, c, t - LAG)
                    elif t and not first:
                        weighted_sum(la, c - 1, NS - LAG + t)
                    scores(la, c, t, shifted)
                    if first and t == LAG - 1:
                        for jb in range(NB):
                            last = nc.tensor.matmul(acc_ps[:, 0, 0:AW], ones_h[:, :], src[la][:, jb, :],
                                                    start=jb == 0, stop=jb == NB - 1)
                        last.then_inc(sums_done[la], 1)
                        pe.wait_ge(sums_out[la], 1)
                if la == 0 and not first:
                    pe.wait_ge(clamped[la] if shifted else exp_done[la], c * NS + (NS - 1))
                    pe.wait_ge(xn_ready[1], c)
                    transposes(1, s_ps[:, 0, 0:CH])
                weighted_sum(la, c, NS - LAG)
                if la == 0 and not first:
                    pe.wait_ge(xt_lo[1], c)

            def attention(la, shifted):
                if shifted:
                    row_maxima(la)
                chunk(la, 0, True, shifted)
                with pe.Fori(1, NC) as c:
                    chunk(la, c, False, shifted)
                for t in range(1, LAG):
                    weighted_sum(la, NC - 1, NS - LAG + t)
                if la == 0:
                    pe.wait_ge(xn_ready[1], NC)
                    transposes(1, s_ps[:, 0, 0:CH])

            pe.wait_ge(flags, 1)
            for la in range(2):
                pe.wait_ge(xt_lo[la], NC)
                pe.wait_ge(consts_made, 7)
                with pe.If(pe.value_load(beta_big[0:1, la:la + 1]) == 0):
                    attention(la, False)
                with pe.Else():
                    attention(la, True)

        @block.scalar
        def _(act):
            act.dma_start(w1[:, 0:F], embed).then_inc(embed_in, 16)
            act.dma_start(eb[:, :], embed_bias.rearrange("(a f) -> a f", a=1).to_broadcast([P, F]))\
                .then_inc(embed_in, 16)
            for dst, s in ((w1[:, F:2 * F], layer[0:F, :]), (w2[:, :], layer[F:2 * F, :]),
                           (lb[:, :], layer_bias.rearrange("(a f) -> a f", a=1).to_broadcast([P, F])),
                           (beta[:, 0:1], beta1.rearrange("(a f) -> a f", a=1).to_broadcast([P, 1])),
                           (beta[:, 1:2], beta2.rearrange("(a f) -> a f", a=1).to_broadcast([P, 1]))):
                act.dma_start(dst, s).then_inc(weights_in, 16)

            asks = [0, 0]

            def on(func, dst, s, **kw):
                asks[1] += 1
                act.wait_ge(asked, asks[0] + asks[1])
                nc.scalar.activation(dst, s, func, **kw).then_inc(told, 1)

            def log_terms(z, plus, minus):
                on(ACT.Ln, plus, z, bias=1.0)
                on(ACT.Ln, minus, z, bias=1.0, scale=-1.0)

            def sm(i, w):
                return small[:, i, 0:w]

            def relu(r):
                act.wait_ge(xs_ready, r + 1)
                nc.scalar.activation(h_sb[:, ts(r, CB), :], scr_b[:, ts(r, CB), :], ACT.Relu).then_inc(h_ready, 1)

            def g_out(r):
                act.wait_ge(g_done, r + 1)
                for b in range(CB):
                    q = r * CB + b
                    nc.scalar.activation(h1_sb[:, q, :], g_ps[r % 2][:, b, :], ACT.Square,
                                         accum_out=small[:, 10, q:q + 1])
                nc.scalar.activation(scr_a[:, ts(r, CB), :], g_ps[r % 2], ACT.Copy).then_inc(g_copied, 1)

            def h1_out(r):
                act.wait_ge(h1_done, r + 1)
                if r == 0:
                    act.wait_ge(g_copied, NC)
                nc.scalar.activation(h1_sb[:, ts(r, CB), :], h1_ps[r % 4], ACT.Copy).then_inc(h1_copied, 1)

            relu(0)
            for r in range(NC):
                if r + 1 < NC:
                    relu(r + 1)
                act.wait_ge(ht_done, r + 1)
                nc.scalar.activation(ht_sb[:, ds(r * CH, CH)], ht_ps[r % 2], ACT.Copy).then_inc(ht_copied, 1)
                if r:
                    g_out(r - 1)
            g_out(NC - 1)
            log_terms(sm(4, NB), sm(5, NB), sm(6, NB))
            on(ACT.Tanh, sm(5, NB), sm(4, NB))
            for r in range(NC // 2):
                h1_out(r)
            log_terms(sm(4, NB), sm(5, NB), sm(6, NB))
            for r in range(NC // 2, NC):
                h1_out(r)
            start = asks[1]

            def split_columns(la, c, ps):
                act.wait_ge(xt_done[la], c + 1)
                nc.scalar.activation(xt[la][:, 0, ds(c * CH, CH)], ps, ACT.Copy).then_inc(xt_hi[la], 1)

            def gnn_chunk(c, parity, first):
                act.wait_ge(agg_tiles, c * NT + NT)
                if first:
                    act.wait_ge(h1_copied, NC)
                else:
                    act.wait_ge(w_done, c)
                nc.scalar.activation(at_sq, acc_ps[:, parity, :], ACT.Square)
                nc.scalar.activation(at_sb, acc_ps[:, parity, :], ACT.Copy).then_inc(at_ready, 1)
                on(ACT.Tanh, sm(5, CB), sm(4, CB))
                log_terms(sm(4, CB), sm(5, CB), sm(6, CB))
                if not first:
                    split_columns(0, c - 1, xt_ps)
                on(ACT.Tanh, sm(5, CB), sm(4, CB))
                on(ACT.Copy, x_sb[:, ds(c * CB, CB), :], t1[:, :, :])
                on(ACT.Copy, src[0][:, ds(c * CB, CB), F:2 * F], t2[:, :, :], scale=FS)

            def turn(c, parity, first):
                asks[0], asks[1] = c * ASKS_CHUNK + start, 0
                gnn_chunk(c, parity, first)
                assert asks[1] == ASKS_CHUNK

            turn(0, 0, True)
            turn(1, 1, False)
            with act.Fori(1, NC // 2) as c2:
                turn(c2 * 2, 0, False)
                turn(c2 * 2 + 1, 1, False)
            split_columns(0, NC - 1, xt_ps)
            asks_gnn = start + NC * ASKS_CHUNK

            def exps(la, c, t, shifted):
                if shifted:
                    act.wait_ge(clamped[la], c * NS + (t + 1))
                    nc.scalar.activation(e_ring[:, t % ER, :], e_ring[:, t % ER, :], ACT.Exp,
                                         bias=p_log[:, 0:1]).then_inc(exp_done[la], 1)
                    return
                act.wait_ge(s_done[la], c * NS + (t + 1))
                wait(act, mask_done[la], c * NS + (t + 1 - ER))
                nc.scalar.activation(e_ring[:, t % ER, :], s_ps[:, t % 2, :], ACT.Exp,
                                     bias=beta_bias[:, la:la + 1], scale=beta_scale[:, la:la + 1])\
                    .then_inc(exp_done[la], 1)

            def p_hi(la, c, t):
                act.wait_ge(mask_done[la], c * NS + (t + 1))
                wait(act, pv_done[la], c * NS + (t + 1 - LAG))
                nc.scalar.activation(ph_ring[:, t % LAG, :], m_ring[:, t % LAG, :], ACT.Copy)\
                    .then_inc(ph_done[la], 1)

            def sums_leave(la, c):
                act.wait_ge(pv_done[la], c * NS + NS)
                nc.scalar.activation(accs[:, :, :], acc_ps[:, :, 0:AW], ACT.Copy).then_inc(acc_out[la], 1)

            def ask_of(la, c, n):
                act.wait_ge(asked, c * ASKS_ROWS[la] + (asks_la[la] + n + 1))

            def averages(la, c):
                ask_of(la, c, 0)
                for b in range(CB):
                    last = nc.scalar.activation(t1[:, b, :], t2[:, b, :], ACT.Copy, scale=small[:, 0, b:b + 1])
                last.then_inc(told, 1)

            def squares(c):
                ask_of(0, c, 1)
                for b in range(CB):
                    last = nc.scalar.activation(t2[:, b, :], t1[:, b, :], ACT.Square,
                                                accum_out=small[:, 2, b:b + 1])
                last.then_inc(told, 1)

            def rows_hi(c):
                nc.scalar.activation(src[1][:, ds(c * CB, CB), F:2 * F], t1[:, :, :], ACT.Copy, scale=FS)\
                    .then_inc(told, 1)

            def normalised(c):
                ask_of(0, c, 2)
                for b in range(CB):
                    last = nc.scalar.activation(t3[:, b, :], t1[:, b, :], ACT.Copy, scale=small[:, 1, b:b + 1])
                last.then_inc(xn_ready[1], 1)

            def chunk(la, c, first, shifted):
                for t in range(NS):
                    if la == 0 and not first and t == NS - 1:
                        split_columns(1, c - 1, s_ps[:, 0, 0:CH])
                    exps(la, c, t, shifted)
                    if la == 0 and not first and t == NS - 2:
                        normalised(c - 1)
                    if not first and t == LAG - 2:
                        sums_leave(la, c - 1)
                    if t:
                        p_hi(la, c, t - 1)
                    elif not first:
                        p_hi(la, c - 1, NS - 1)
                    if first and t == LAG - 1:
                        act.wait_ge(sums_done[la], 1)
                        nc.scalar.activation(fallback[:, :], acc_ps[:, 0, 0:AW], ACT.Copy).then_inc(sums_out[la], 1)
                    if not first and t == LAG:
                        averages(la, c - 1)
                    if la == 0 and not first and t == LAG + 2:
                        squares(c - 1)
                    if la == 0 and not first and t == LAG + 3:
                        rows_hi(c - 1)

            def attention(la, shifted):
                chunk(la, 0, True, shifted)
                with act.Fori(1, NC) as c:
                    chunk(la, c, False, shifted)
                p_hi(la, NC - 1, NS - 1)
                sums_leave(la, NC - 1)
                averages(la, NC - 1)
                if la == 0:
                    squares(NC - 1)
                    rows_hi(NC - 1)
                    normalised(NC - 1)
                    split_columns(1, NC - 1, s_ps[:, 0, 0:CH])

            asks_la = [asks_gnn, asks_gnn + NC * ASKS_ROWS[0]]
            act.wait_ge(flags, 1)
            for la in range(2):
                with act.If(act.value_load(beta_big[0:1, la:la + 1]) == 0):
                    attention(la, False)
                with act.Else():
                    attention(la, True)

        @block.vector
        def _(dve):
            step = Chain(dve, vec)
            answers, asks = [0, 0], [0]
            V = nc.vector

            def ask(ins, n=1):
                ins.then_inc(asked, n)
                asks[0] += n
                dve.wait_ge(asked, answers[0] + asks[0])

            def answered(n=1):
                answers[1] += n
                dve.wait_ge(told, answers[0] + answers[1])

            def sm(i, w):
                return small[:, i, 0:w]

            def total(dst, s):
                step(V.tensor_reduce(dst, s, axis=AX.X, op=ALU.add))

            def inv_sqrt(y, v, t):
                step(V.tensor_scalar(y.bitcast(i32), v.bitcast(i32), 1, None, ALU.logical_shift_right))
                step(V.tensor_scalar(y.bitcast(i32), y.bitcast(i32), -1.0, float(0x5F3759DF), ALU.mult, ALU.add))
                for _ in range(3):
                    step(V.tensor_tensor(t, y, y, ALU.mult))
                    step(V.scalar_tensor_tensor(t, t, -0.5, v, ALU.mult, ALU.mult))
                    step(V.scalar_tensor_tensor(y, t, 1.5, y, ALU.add, ALU.mult))

            def norm(n, rn, squares, eps, w):
                v, t = sm(14, w), sm(15, w)
                step(V.tensor_scalar(v, squares, TINY, None, ALU.max))
                inv_sqrt(rn, v, t)
                V.tensor_tensor(n, rn, v, ALU.mult)
                step(V.tensor_scalar(rn, rn, 1.0 / eps, None, ALU.min))
                step(V.tensor_scalar(n, n, eps, None, ALU.max))

            def atanh_over(c, n, rn, w):
                z, lp, lm, u, s = (sm(i, w) for i in (4, 5, 6, 7, 8))
                ask(V.tensor_scalar(z, n, MAX_TANH, None, ALU.min), 2)
                step(V.tensor_tensor(u, z, z, ALU.mult))
                step(V.tensor_scalar(s, u, 1.0 / 13, None, ALU.mult))
                for k in (11, 9, 7, 5, 3):
                    step(V.scalar_tensor_tensor(s, s, 1.0 / k, u, ALU.add, ALU.mult))
                step(V.scalar_tensor_tensor(s, s, 1.0, z, ALU.add, ALU.mult))
                answered(2)
                step(V.tensor_tensor(lp, lp, lm, ALU.subtract))
                step(V.scalar_tensor_tensor(s, lp, -0.5, s, ALU.mult, ALU.add))
                step(V.tensor_scalar(u, z, SERIES, None, ALU.is_lt))
                step(V.tensor_tensor(s, s, u, ALU.mult))
                step(V.scalar_tensor_tensor(s, lp, 0.5, s, ALU.mult, ALU.add))
                step(V.tensor_tensor(c, s, rn, ALU.mult))

            def product_scalars(nw, c, gb, ww, y, w):
                z, th, den, al, xy, x2 = (sm(i, w) for i in (4, 5, 6, 11, 12, 13))
                step(V.tensor_tensor(z, nw, c, ALU.mult))
                ask(V.tensor_scalar(z, z, EPS, None, ALU.max))
                step(V.reciprocal(al, z))
                step(V.tensor_tensor(al, al, c, ALU.mult))
                answered()
                step(V.tensor_tensor(al, al, th, ALU.mult))
                V.tensor_tensor(xy, al, gb, ALU.mult)
                step(V.tensor_tensor(x2, al, al, ALU.mult))
                V.tensor_scalar(xy, xy, 2.0, 1.0, ALU.mult, ALU.add)
                step(V.tensor_tensor(x2, x2, ww, ALU.mult))
                step(V.scalar_tensor_tensor(den, x2, y, xy, ALU.mult, ALU.add))
                step(V.tensor_scalar(den, den, EPS, None, ALU.max))
                V.scalar_tensor_tensor(xy, xy, y, al, ALU.add, ALU.mult)
                step(V.reciprocal(den, den))
                V.tensor_scalar(x2, x2, -1.0, 1.0, ALU.mult, ALU.add)
                step(V.tensor_tensor(xy, xy, den, ALU.mult))
                step(V.tensor_tensor(x2, x2, den, ALU.mult))

            def blocks(r):
                return range(r * CB, (r + 1) * CB)

            for i in range(XP):
                dve.wait_ge(x_in[i], 16)
                for b in range(i * NB // XP, (i + 1) * NB // XP):
                    ins = V.bn_stats(stats[:, b, :], x_sb[:, b, :])
                step(ins)
                V.memset(sm(0, NB), 0.0)
                for b in range(i * NB // XP, (i + 1) * NB // XP):
                    ins = V.bn_aggr(mean_var[:, b, :], stats[:, b, :])
            step(ins)
            step(V.tensor_scalar(sm(0, NB), mean_var[:, :, 1], LN_EPS, None, ALU.add))
            inv_sqrt(sm(1, NB), sm(0, NB), sm(2, NB))
            for r in range(NC):
                for b in blocks(r):
                    ins = V.tensor_scalar(scr_b[:, b, :], x_sb[:, b, :], mean_var[:, b, 0:1], small[:, 1, b:b + 1],
                                          ALU.subtract, ALU.mult)
                ins.then_inc(xs_ready, 1)
            dve.wait_ge(xs_ready, NC)
            dve.wait_ge(embed_in, 16 * 2)
            V.scalar_tensor_tensor(bsq[:, :], w1[:, 0:F], 1.0, eb[:, :], ALU.mult, ALU.mult,
                                   accum_out=web[:, :]).then_inc(web_made, 1)
            dve.wait_ge(weights_in, 16 * 5)
            for i, b in enumerate((eb, lb)):
                dve.wait_ge(web_made, i + 1)
                V.scalar_tensor_tensor(bsq[:, :], b[:, :], 1.0, b[:, :], ALU.mult, ALU.mult,
                                       accum_out=y2[:, i:i + 1]).then_inc(web_made, 1)
            for b in range(NB):
                ins = V.scalar_tensor_tensor(v_sb[:, b, :], scr_b[:, b, :], 0.0, scr_b[:, b, :],
                                             ALU.max, ALU.mult, accum_out=hh[:, b:b + 1])
            step(ins)
            norm(sm(0, NB), sm(1, NB), hh[:, :], EPS, NB)
            atanh_over(sm(2, NB), sm(0, NB), sm(1, NB), NB)
            dve.wait_ge(g_copied, NC)
            norm(sm(0, NB), sm(1, NB), sm(10, NB), EPS, NB)
            dve.wait_ge(gb_done, 1)
            product_scalars(sm(0, NB), sm(2, NB), gb_ps, sm(10, NB), y2[:, 0:1], NB)
            xy, x2, rr, cross = (sm(i, NB) for i in (12, 13, 3, 9))
            V.tensor_tensor(rr, xy, xy, ALU.mult)
            V.tensor_tensor(cross, xy, gb_ps, ALU.mult)
            step(V.tensor_scalar(sm(7, NB), x2, y2[:, 0:1], None, ALU.mult))
            V.tensor_tensor(rr, rr, sm(10, NB), ALU.mult)
            step(V.scalar_tensor_tensor(cross, cross, 2.0, sm(7, NB), ALU.mult, ALU.add))
            step(V.tensor_tensor(cross, cross, x2, ALU.mult))
            step(V.tensor_tensor(rr, rr, cross, ALU.add))
            norm(sm(0, NB), sm(1, NB), rr, EPS, NB)
            atanh_over(sm(2, NB), sm(0, NB), sm(1, NB), NB)
            V.tensor_tensor(xy, xy, sm(2, NB), ALU.mult)
            step(V.tensor_tensor(x2, x2, sm(2, NB), ALU.mult))
            V.tensor_scalar(scr_b[:, 0, :], eb[:, :], small[:, 13, 0:1], None, ALU.mult).then_inc(bias_part, 1)
            for b in range(NB):
                if b + 1 < NB:
                    V.tensor_scalar(scr_b[:, b + 1, :], eb[:, :], small[:, 13, b + 1:b + 2], None, ALU.mult)\
                        .then_inc(bias_part, 1)
                dve.wait_ge(bias_part, b + 1)
                V.scalar_tensor_tensor(v_sb[:, b, :], scr_a[:, b, :], small[:, 12, b:b + 1],
                                       scr_b[:, b, :], ALU.mult, ALU.add).then_inc(v_ready, 1)
            step(V.tensor_scalar(beta_nsign[:, :], beta[:, :], -1.0, None, ALU.mult))
            step(V.tensor_tensor(beta_abs[:, :], beta[:, :], beta_nsign[:, :], ALU.max))
            step(V.tensor_scalar(beta_scale[:, :], beta[:, :], 1.0 / FS ** 2, None, ALU.mult))
            step(V.tensor_scalar(beta_bias[:, :], beta_abs[:, :], -1.0, P_LOG, ALU.mult, ALU.add))
            step(V.tensor_scalar(beta_sign[:, :], beta[:, :], 0.0, None, ALU.is_ge))
            step(V.tensor_scalar(beta_sign[:, :], beta_sign[:, :], 2.0, -1.0, ALU.mult, ALU.add))
            step(V.tensor_scalar(beta_nsign[:, :], beta_sign[:, :], -1.0, None, ALU.mult))
            V.tensor_scalar(beta_big[:, :], beta_abs[:, :], BETA_MAX, None, ALU.is_gt).then_inc(flags, 1)
            assert asks[0] == answers[1]
            start = answers[1]
            steps_start = step.n

            def split_columns(la, c, ps):
                dve.wait_ge(xt_hi[la], c + 1)
                V.tensor_tensor(xt[la][:, 1, ds(c * CH, CH)], ps, xt[la][:, 0, ds(c * CH, CH)], ALU.subtract)\
                    .then_inc(xt_lo[la], 1)

            def gnn_chunk(c, first):
                rows = ds(c * CB, CB)
                both, squares = slice(CB, 2 * CB), small[:, 2, 0:2 * CB]
                dve.wait_ge(w_done, c + 1)
                norm(sm(4, CB), sm(1, CB), n_ps, EPS, CB)
                ask(V.tensor_copy(sm(4, CB), sm(4, CB)))
                answered()
                step(V.tensor_tensor(sm(3, CB), sm(5, CB), sm(1, CB), ALU.mult))
                for b in range(CB):
                    ins = V.scalar_tensor_tensor(t1[:, b, :], w_ps[:, b, :], small[:, 3, b:b + 1],
                                                 h1_sb[:, c * CB + b, :], ALU.mult, ALU.add)
                step(ins)
                V.tensor_tensor(sm(7, CB), sm(3, CB), sm(3, CB), ALU.mult)
                for b in range(CB):
                    ins = V.scalar_tensor_tensor(t2[:, b, :], t1[:, b, :], 1.0, t1[:, b, :], ALU.mult, ALU.mult,
                                                 accum_out=small[:, 2, CB + b:CB + b + 1])
                step(ins)
                V.tensor_tensor(sm(7, CB), sm(7, CB), n_ps, ALU.mult)
                for b in range(CB):
                    ins = V.scalar_tensor_tensor(t2[:, b, :], t1[:, b, :], 1.0, lb[:, :], ALU.mult, ALU.mult,
                                                 accum_out=small[:, 9, b:b + 1])
                step(ins)
                V.tensor_copy(sm(10, CB), small[:, 2, both]).then_inc(w_read, 1)
                dve.wait_ge(w_read, c + 1)
                step(V.tensor_tensor(small[:, 2, 0:CB], sm(7, CB), hh[:, rows], ALU.add))
                norm(sm(0, 2 * CB), sm(1, 2 * CB), squares, EPS, 2 * CB)
                atanh_over(sm(2, CB), sm(0, CB), sm(1, CB), CB)
                if not first:
                    split_columns(0, c - 1, xt_ps)
                product_scalars(small[:, 0, both], sm(2, CB), sm(9, CB), sm(10, CB), y2[:, 1:2], CB)
                for b in range(CB):
                    ins = V.tensor_scalar(t2[:, b, :], lb[:, :], small[:, 13, b:b + 1], None, ALU.mult)
                step(ins)
                for b in range(CB):
                    ins = V.scalar_tensor_tensor(t1[:, b, :], t1[:, b, :], small[:, 12, b:b + 1], t2[:, b, :],
                                                 ALU.mult, ALU.add)
                step(ins)
                ask(V.tensor_tensor(t1[:, :, :], x_sb[:, rows, :], t1[:, :, :], ALU.add))
                for b in range(CB):
                    ins = V.bn_stats(stats[:, b, :], t1[:, b, :])
                step(ins)
                V.memset(sm(0, CB), 0.0)
                for b in range(CB):
                    ins = V.bn_aggr(mean_var[:, b, :], stats[:, b, :])
                step(ins)
                V.tensor_scalar(small[:, 2, 0:CB], mean_var[:, 0:CB, 1], LN_EPS, None, ALU.add)
                for b in range(CB):
                    ins = V.tensor_scalar(t2[:, b, :], t1[:, b, :], mean_var[:, b, 0:1], None, ALU.subtract)
                step(ins)
                for b in range(CB):
                    ins = V.scalar_tensor_tensor(t3[:, b, :], t2[:, b, :], 0.0, t2[:, b, :], ALU.max, ALU.mult,
                                                 accum_out=small[:, 2, CB + b:CB + b + 1])
                step(ins)
                step(V.tensor_scalar(squares, squares, TINY, None, ALU.max))
                inv_sqrt(sm(1, 2 * CB), squares, sm(3, 2 * CB))
                for b in range(CB):
                    ins = V.tensor_scalar(t2[:, b, :], t2[:, b, :], 0.0, small[:, 1, b:b + 1], ALU.max, ALU.mult)
                ask(ins)
                V.tensor_tensor(sm(0, CB), small[:, 1, both], small[:, 2, both], ALU.mult)
                answered(2)
                step(V.scalar_tensor_tensor(src[0][:, rows, 0:F], t2[:, :, :], FS, src[0][:, rows, F:2 * F],
                                            ALU.mult, ALU.subtract))
                step(V.tensor_tensor(sm(0, CB), sm(0, CB), sm(1, CB), ALU.mult))
                step(V.tensor_scalar(sm(0, CB), sm(0, CB), NORM_EPS, None, ALU.max))
                step(V.reciprocal(sm(1, CB), sm(0, CB)))
                for b in range(CB):
                    ins = V.tensor_scalar(t3[:, b, :], t2[:, b, :], small[:, 1, b:b + 1], FS, ALU.mult, ALU.mult)
                ins.then_inc(xn_ready[0], 1)

            STEPS = 80

            def gnn_turn(c, first):
                step.base, step.n = c * STEPS + steps_start, 0
                answers[0], answers[1], asks[0] = c * ASKS_CHUNK + start, 0, 0
                gnn_chunk(c, first)
                assert step.n == STEPS and answers[1] == ASKS_CHUNK, (step.n, answers[1])

            gnn_turn(0, True)
            with dve.Fori(1, NC) as c:
                gnn_turn(c, False)
            split_columns(0, NC - 1, xt_ps)
            steps_gnn = steps_start + NC * STEPS
            asks_gnn = start + NC * ASKS_CHUNK

            tile_base = [16 * NC * (1 + la) for la in range(2)]

            def clamp(la, c, t):
                dve.wait_ge(s_done[la], c * NS + (t + 1))
                wait(dve, mask_done[la], c * NS + (t + 1 - ER))
                V.tensor_scalar(e_ring[:, t % ER, :], s_ps[:, t % 2, :], beta_scale[:, la:la + 1], 0.0,
                                ALU.mult, ALU.min).then_inc(clamped[la], 1)

            def mask(la, c, t):
                k, half_tile = t * SB // TB, t * SB % TB
                dve.wait_ge(exp_done[la], c * NS + (t + 1))
                if half_tile == 0:
                    dve.wait_ge(tile_in[k], 16 * c + (tile_base[la] + 16))
                wait(dve, pl_done[la], c * NS + (t + 1 - LAG))
                V.scalar_tensor_tensor(m_ring[:, t % LAG, :], ring[:, k, half_tile:half_tile + SB, :]
                                       .rearrange("p b i -> p (b i)"), 0.0, e_ring[:, t % ER, :],
                                       ALU.is_gt, ALU.mult).then_inc(mask_done[la], 1)

            def p_lo(la, c, t):
                dve.wait_ge(ph_done[la], c * NS + (t + 1))
                wait(dve, pv_done[la], c * NS + (t + 1 - LAG))
                V.tensor_tensor(pl_ring[:, t % LAG, :], m_ring[:, t % LAG, :], ph_ring[:, t % LAG, :],
                                ALU.subtract).then_inc(pl_done[la], 1)

            def averages(la, c):
                step.base, step.n = c * ROWS[la] + steps_la[la], 0
                den = accs[:, :, 2 * F]
                dve.wait_ge(acc_out[la], c + 1)
                V.tensor_scalar(zero[:, :], den, 0.0, None, ALU.is_equal)
                step(V.tensor_scalar(sm(1, CB), den, TINY, None, ALU.max))
                step(V.reciprocal(sm(0, CB), sm(1, CB)))
                V.tensor_tensor(t2[:, :, :], accs[:, :, 0:F], accs[:, :, F:2 * F], ALU.add).then_inc(asked, 1)

            def leaky(la, c):
                dve.wait_ge(told, c * TOLD_ROWS[la] + (told_la[la] + 1))
                for b in range(CB):
                    ins = V.scalar_tensor_tensor(t1[:, b, :], mean_row[:, :], zero[:, b:b + 1], t1[:, b, :],
                                                 ALU.mult, ALU.add)
                step(ins)
                ins = V.scalar_tensor_tensor(t1[:, :, :], t1[:, :, :], LEAK, t1[:, :, :], ALU.mult, ALU.max)
                if la == 0:
                    ins.then_inc(asked, 1)
                else:
                    step(ins)
                    rows = ds(c * CB, CB)
                    V.tensor_tensor(x_sb[:, rows, :], x_sb[:, rows, :], t1[:, :, :], ALU.add).then_inc(out_ready, 1)

            def rows_lo(c):
                rows = ds(c * CB, CB)
                dve.wait_ge(told, c * TOLD_ROWS[0] + (told_la[0] + 3))
                V.scalar_tensor_tensor(src[1][:, rows, 0:F], t1[:, :, :], FS, src[1][:, rows, F:2 * F],
                                       ALU.mult, ALU.subtract)

            NORM_PARTS = 13

            def norm_part(la_c, i):
                v, y, w = sm(2, CB), sm(1, CB), sm(3, CB)
                if i == 0:
                    dve.wait_ge(told, la_c * TOLD_ROWS[0] + (told_la[0] + 2))
                else:
                    dve.wait_ge(vec, la_c * ROWS[0] + (steps_la[0] + ROWS[0] - NORM_PARTS + 1 + i))
                if i == 0:
                    ins = V.tensor_scalar(v, v, TINY, None, ALU.max)
                elif i == 1:
                    ins = V.tensor_scalar(y.bitcast(i32), v.bitcast(i32), 1, None, ALU.logical_shift_right)
                elif i == 2:
                    ins = V.tensor_scalar(y.bitcast(i32), y.bitcast(i32), -1.0, float(0x5F3759DF),
                                          ALU.mult, ALU.add)
                elif i == NORM_PARTS - 1:
                    V.tensor_scalar(y, y, 1.0 / NORM_EPS, FS, ALU.min, ALU.mult).then_inc(asked, 1)
                    return
                elif i % 3 == 0:
                    ins = V.tensor_tensor(w, y, y, ALU.mult)
                elif i % 3 == 1:
                    ins = V.scalar_tensor_tensor(w, w, -0.5, v, ALU.mult, ALU.mult)
                else:
                    ins = V.scalar_tensor_tensor(y, w, 1.5, y, ALU.add, ALU.mult)
                ins.then_inc(vec, 1)
                step.n += 1

            ROWS = (3 + NORM_PARTS - 1, 4)
            TOLD_ROWS = (3, 1)
            steps_la = [steps_gnn, steps_gnn + NC * ROWS[0]]
            told_la = [asks_gnn, asks_gnn + NC * TOLD_ROWS[0]]

            def chunk(la, c, first, shifted):
                for t in range(NS):
                    between = la == 0 and not first
                    if between and t == NS - 1:
                        split_columns(1, c - 1, s_ps[:, 0, 0:CH])
                    if shifted:
                        if t == 0 and not first:
                            shift_rows(la, c)
                        clamp(la, c, t)
                    mask(la, c, t)
                    if between and LAG + 3 <= t <= LAG + 8:
                        norm_part(c - 1, 2 * (t - LAG - 3))
                    if t:
                        p_lo(la, c, t - 1)
                    elif not first:
                        p_lo(la, c - 1, NS - 1)
                    if not first and t == LAG - 1:
                        averages(la, c - 1)
                    if not first and t == LAG + 1:
                        leaky(la, c - 1)
                    if between and LAG + 3 <= t <= LAG + 8:
                        norm_part(c - 1, 2 * (t - LAG - 3) + 1)
                    if between and t == LAG + 8:
                        norm_part(c - 1, NORM_PARTS - 1)
                    if between and t == LAG + 9:
                        rows_lo(c - 1)
                    if first and t == LAG:
                        dve.wait_ge(sums_out[la], 1)
                        V.tensor_tensor(mean_row[:, :], fallback[:, 0:F], fallback[:, F:2 * F], ALU.add)\
                            .then_inc(mean_made, 1)
                        dve.wait_ge(mean_made, la + 1)
                        V.tensor_scalar(mean_row[:, :], mean_row[:, :], 1.0 / (N * FS), None, ALU.mult)
                if not first:
                    assert step.n == ROWS[la], step.n

            def shift_rows(la, c):
                wait(dve, s_done[la], c * NS)
                V.tensor_tensor(neg_rows[:, :, :], neg_t[:, :].unsqueeze(1).to_broadcast([NB, CB, P]),
                                ident[0:NB, ds(c * CB, CB)].unsqueeze(2).to_broadcast([NB, CB, P]),
                                ALU.mult).then_inc(shift_ready[la], 1)

            def row_maxima(la):
                with dve.Fori(0, NB) as b:
                    dve.wait_ge(rows_in[la], b * 16 + 16)
                    for j in range(NC):
                        V.tensor_scalar(t1[:, :, :].rearrange("p b f -> p (b f)"), adj_rows[:, ts(j, CH)],
                                        0.0, -1e9, ALU.is_le, ALU.mult).then_inc(max_step[la], 1)
                        dve.wait_ge(max_step[la], b * (2 * NC) + (2 * j + 1))
                        dve.wait_ge(sm_done[la], b * NC + (j + 1))
                        V.scalar_tensor_tensor(t2[:, :, :].rearrange("p b f -> p (b f)"), s_ps[:, 0, 0:CH],
                                               beta_sign[:, la:la + 1], t1[:, :, :].rearrange("p b f -> p (b f)"),
                                               ALU.mult, ALU.add).then_inc(max_step[la], 1)
                        dve.wait_ge(max_step[la], b * (2 * NC) + (2 * j + 2))
                        V.tensor_reduce(ext8[:, j:j + 1], t2[:, :, :].rearrange("p b f -> p (b f)"),
                                        axis=AX.X, op=ALU.max).then_inc(sm_read[la], 1)
                    dve.wait_ge(sm_read[la], b * NC + NC)
                    V.tensor_reduce(ext[:, ds(b, 1)], ext8[:, :], axis=AX.X, op=ALU.max).then_inc(rows_used[la], 1)
                dve.wait_ge(rows_used[la], NB)
                V.tensor_scalar(ext[:, :], ext[:, :], -2.0 * FS ** 2, beta_nsign[:, la:la + 1],
                                ALU.max, ALU.mult).then_inc(neg_ready[la], 1)
                dve.wait_ge(neg_done[la], 1)
                V.tensor_copy(neg_t[:, :], s_ps[0:NB, 1, 0:P]).then_inc(neg_ready[la], 1)
                dve.wait_ge(neg_ready[la], 2)

            def attention(la, shifted):
                if shifted:
                    row_maxima(la)
                    shift_rows(la, 0)
                chunk(la, 0, True, shifted)
                with dve.Fori(1, NC) as c:
                    chunk(la, c, False, shifted)
                p_lo(la, NC - 1, NS - 1)
                averages(la, NC - 1)
                leaky(la, NC - 1)
                if la == 0:
                    for i in range(NORM_PARTS):
                        norm_part(NC - 1, i)
                    rows_lo(NC - 1)
                    split_columns(1, NC - 1, s_ps[:, 0, 0:CH])

            dve.wait_ge(flags, 1)
            for la in range(2):
                with dve.If(dve.value_load(beta_big[0:1, la:la + 1]) == 0):
                    attention(la, False)
                with dve.Else():
                    attention(la, True)


def kernel(x, adj, L0_gnn_embed, L0_gnn_layer, L0_gnn_embed_bias, L0_gnn_layer_bias, L1_gnn_beta1, L1_gnn_beta2):
    import concourse.bacc as bacc
    from concourse.bass_utils import run_bass_kernel_spmd

    arrays = {"x": x, "adj": adj, "adj_t": np.asarray(adj).T, "embed": L0_gnn_embed, "layer": L0_gnn_layer,
              "embed_bias": L0_gnn_embed_bias, "layer_bias": L0_gnn_layer_bias,
              "beta1": L1_gnn_beta1, "beta2": L1_gnn_beta2}
    arrays = {f"in_{k}": np.ascontiguousarray(a) for k, a in arrays.items()}
    nc = bacc.Bacc("TRN2", target_bir_lowering=False, num_devices=1)
    args = [nc.dram_tensor(k, a.shape, mybir.dt.float32, kind="ExternalInput").ap() for k, a in arrays.items()]
    out = nc.dram_tensor("out_0", arrays["in_x"].shape, mybir.dt.float32, kind="ExternalOutput").ap()
    build(nc, *args, out)
    return run_bass_kernel_spmd(nc, [arrays], core_ids=[0]).results[0]["out_0"]
```

```python
import numpy as np
import concourse.bass as bass
import concourse.mybir as mybir
from contextlib import ExitStack


def build(nc, x, adj, adj_t, embed, layer, embed_bias, layer_bias, beta1, beta2, out):
    f32, f16, i32 = mybir.dt.float32, mybir.dt.float16, mybir.dt.int32
    ACT, ALU, AX = mybir.ActivationFunctionType, mybir.AluOpType, mybir.AxisListType
    ts, ds = bass.ts, bass.ds

    N, F = x.shape
    P = 128
    NB = N // P
    CH = 512
    CB = CH // P
    NC = N // CH
    TB = 4
    NT = NB // TB
    SB = 2
    NS = NB // SB
    ER = 2
    LAG = 4
    AW = 2 * F + 1
    XP = 4
    EPS, MAX_TANH, LN_EPS, NORM_EPS, LEAK = 1e-7, 1.0 - 1e-6, 1e-5, 1e-12, 0.3
    TINY = 1e-30
    FS = 256.0
    P_LOG = 15 * float(np.log(2.0))
    BETA_MAX = 4.0
    SERIES = 0.25

    ctx = ExitStack()
    with ctx:
        def sb(name, shape, dt=f32):
            return ctx.enter_context(nc.sbuf_tensor(name, shape, dt))

        def sem(name):
            return ctx.enter_context(nc.semaphore(name))

        ring = sb("ring", [P, NT, TB, CH])
        x_sb = sb("x_sb", [P, NB, F])
        h_all = sb("h_all", [P, max(NB * F, LAG * SB * CH)])
        h_sb = h_all[:, 0:NB * F].rearrange("p (b f) -> p b f", f=F)
        p_rings = h_all[:, 0:LAG * SB * CH].bitcast(f16).rearrange("p (s r n) -> p s r n", s=2, r=LAG)
        ph_ring, pl_ring = p_rings[:, 0], p_rings[:, 1]
        set1 = sb("set1", [P, 2 * NB * F + NB])
        v_sb = set1[:, 0:NB * F].rearrange("p (b f) -> p b f", f=F)
        h1_sb = set1[:, NB * F:2 * NB * F].rearrange("p (b f) -> p b f", f=F)
        set1_h = set1[:, :].bitcast(f16)
        src0_all = sb("src0", [P, NB * AW], f16)
        src0 = src0_all[:, :].rearrange("p (b w) -> p b w", w=AW)
        xt0 = sb("xt0", [F, 2, N], f16)
        src = [src0, set1_h[:, 2 * N:2 * N + NB * AW].rearrange("p (b w) -> p b w", w=AW)]
        xt = [xt0, set1_h[:, 0:2 * N].rearrange("p (s n) -> p s n", s=2)]

        work = sb("work", [P, (ER + LAG) * SB * CH])
        e_ring = work[:, 0:ER * SB * CH].rearrange("p (r n) -> p r n", r=ER)
        m_ring = work[:, ER * SB * CH:(ER + LAG) * SB * CH].rearrange("p (r n) -> p r n", r=LAG)
        adj_rows = work[:, 0:N]
        scr_a = work[:, 0:NB * F].rearrange("p (b f) -> p b f", f=F)
        scr_b = xt0[:, :, :].rearrange("p s n -> p (s n)").bitcast(f32)[:, 0:NB * F].rearrange("p (b f) -> p b f", f=F)
        accs = sb("accs", [P, CB, AW])
        col_sums = sb("col_sums", [P, 2, AW])
        mean_row = sb("mean_row", [P, F])
        t1 = sb("t1", [P, CB, F])
        t2 = sb("t2", [P, CB, F])
        t3 = sb("t3", [P, CB, F])
        at_sb = accs[:, :, :].rearrange("p b w -> p (b w)")[:, 0:CH]
        at_sq = accs[:, :, :].rearrange("p b w -> p (b w)")[:, CH:2 * CH]

        w1 = sb("w1", [F, 2 * F])
        w2 = sb("w2", [F, F])
        eb = sb("eb", [P, F])
        lb = sb("lb", [P, F])
        bsq = sb("bsq", [P, F])
        y2 = sb("y2", [P, 2])
        beta = sb("beta", [P, 2])
        beta_abs = sb("beta_abs", [P, 2])
        beta_big = sb("beta_big", [P, 2], i32)
        beta_scale = sb("beta_scale", [P, 2])
        beta_bias = sb("beta_bias", [P, 2])
        beta_sign = sb("beta_sign", [P, 2])
        beta_nsign = sb("beta_nsign", [P, 2])
        p_log = sb("p_log", [P, 1])
        ident = sb("ident", [P, P])
        ones = sb("ones", [P, P])
        ht_sb = src0_all[:, 0:2 * N].bitcast(f32)
        web = sb("web", [F, 1])
        ones_h = sb("ones_h", [P, P], f16)
        small = sb("small", [P, 16, NB])
        hh = sb("hh", [P, NB])
        zero = sb("zero", [P, CB])
        neg_t = sb("neg_t", [NB, P])
        neg_rows = sb("neg_rows", [NB, CB, P])
        stats = sb("stats", [P, NB, 6])
        mean_var = sb("mean_var", [P, NB, 2])
        ext = sb("ext", [P, NB])
        ext8 = sb("ext8", [P, NC])

        s_ps = ctx.enter_context(nc.psum_tensor("s_ps", [P, 2, SB * CH], f32))
        acc_ps = ctx.enter_context(nc.psum_tensor("acc_ps", [P, CB, 512], f32))
        g_ps = [s_ps[:, i, 0:CH].rearrange("p (b f) -> p b f", f=F) for i in range(2)]
        h1_ps = [s_ps[:, i // 2, ts(i % 2, CH)].rearrange("p (b f) -> p b f", f=F) for i in range(4)]
        gb_ps = acc_ps[:, 0, 0:NB]
        w_ps = s_ps[:, 0, 0:CH].rearrange("p (b f) -> p b f", f=F)
        xt_ps = s_ps[:, 1, 0:CH]
        ht_ps = [acc_ps[:, 2 + i, :] for i in range(2)]
        n_ps = acc_ps[:, 2, 0:CB]
        w_last_ps = acc_ps[:, 3, :].rearrange("p (b f) -> p b f", f=F)
        xt_before_ps = acc_ps[:, 0, :]
        slot_ps = s_ps[:, 0, 0:CH]
        early_ps = acc_ps[:, 1, 0:AW]

        x_in = [sem(f"x_in{i}") for i in range(XP)]
        embed_in = sem("embed_in")
        weights_in = sem("weights_in")
        consts_made = sem("consts_made")
        tile_in = [sem(f"tile_in{k}") for k in range(NT)]
        agg_tiles = sem("agg_tiles")
        vec = sem("vec")
        asked = sem("asked")
        told = sem("told")
        flags = sem("flags")
        mean_made = sem("mean_made")
        xs_ready = sem("xs_ready")
        h_ready = sem("h_ready")
        web_made = sem("web_made")
        ht_done = sem("ht_done")
        ht_copied = sem("ht_copied")
        g_done = sem("g_done")
        gb_done = sem("gb_done")
        h1_done = sem("h1_done")
        g_copied = sem("g_copied")
        h1_copied = sem("h1_copied")
        v_ready = sem("v_ready")
        bias_part = sem("bias_part")
        at_ready = sem("at_ready")
        w_done = sem("w_done")
        w_read = sem("w_read")
        xn_ready = [sem(f"xn_ready{i}") for i in range(2)]
        xt_done = [sem(f"xt_done{i}") for i in range(2)]
        xt_hi = [sem(f"xt_hi{i}") for i in range(2)]
        xt_lo = [sem(f"xt_lo{i}") for i in range(2)]
        s_done = [sem(f"s_done{i}") for i in range(2)]
        exp_done = [sem(f"exp_done{i}") for i in range(2)]
        mask_done = [sem(f"mask_done{i}") for i in range(2)]
        ph_done = [sem(f"ph_done{i}") for i in range(2)]
        pl_done = [sem(f"pl_done{i}") for i in range(2)]
        pl_early = sem("pl_early")
        pv_done = [sem(f"pv_done{i}") for i in range(2)]
        acc_out = [sem(f"acc_out{i}") for i in range(2)]
        summed = [sem(f"summed{i}") for i in range(2)]
        sums_done = [sem(f"sums_done{i}") for i in range(2)]
        sums_out = [sem(f"sums_out{i}") for i in range(2)]
        clamped = [sem(f"clamped{i}") for i in range(2)]
        rows_in = [sem(f"rows_in{i}") for i in range(2)]
        rows_used = [sem(f"rows_used{i}") for i in range(2)]
        sm_done = [sem(f"sm_done{i}") for i in range(2)]
        sm_read = [sem(f"sm_read{i}") for i in range(2)]
        neg_done = [sem(f"neg_done{i}") for i in range(2)]
        neg_ready = [sem(f"neg_ready{i}") for i in range(2)]
        shift_ready = [sem(f"shift_ready{i}") for i in range(2)]
        max_step = [sem(f"max_step{i}") for i in range(2)]
        out_ready = sem("out_ready")
        stored = sem("stored")

        adj_tiles = adj_t.rearrange("(t b p) i -> t p b i", b=TB, p=P)
        x_v = x.rearrange("(b p) f -> p b f", p=P)
        out_v = out.rearrange("(b p) f -> p b f", p=P)
        adj_v = adj.rearrange("(b p) j -> b p j", p=P)

        def wait(eng, s, value):
            if not isinstance(value, int) or value > 0:
                eng.wait_ge(s, value)

        class Chain:
            def __init__(self, eng, s):
                self.eng, self.s, self.base, self.n = eng, s, 0, 0

            def __call__(self, ins):
                ins.then_inc(self.s, 1)
                self.n += 1
                self.eng.wait_ge(self.s, self.base + self.n)

        def wait_p_lo(eng, la, n, joined):
            if joined and n <= PAUSES:
                wait(eng, pl_early, n)
            else:
                wait(eng, pl_done[la], n)

        def c_last(c):
            return isinstance(c, int) and c == NC - 1

        PAUSES = 12
        LAST_SOURCES = (NC - 1) * CB // SB
        assert PAUSES < LAST_SOURCES
        ASKS_CHUNK = 5
        ASKS_ROWS = (3, 1)
        block = ctx.enter_context(nc.Block())

        @block.sync
        def _(sp):
            for i in range(XP):
                sp.dma_start(x_sb[:, ts(i, NB // XP), :], x_v[:, ts(i, NB // XP), :]).then_inc(x_in[i], 16)

            def load(k, c):
                sp.dma_start(ring[:, k, :, :], adj_tiles[k, :, :, ds(c * CH, CH)]).then_inc(tile_in[k], 16)

            for k in range(NT):
                load(k, 0)
            with sp.Fori(1, NC) as c:
                for k in range(NT):
                    sp.wait_ge(agg_tiles, (c - 1) * NT + (k + 1))
                    load(k, c)
            for la in range(2):
                for k in range(NT):
                    if la == 0:
                        sp.wait_ge(agg_tiles, (NC - 1) * NT + (k + 1))
                    else:
                        sp.wait_ge(mask_done[0], (NC - 1) * NS + 2 * k + 2)
                    load(k, 0)
                with sp.Fori(1, NC) as c:
                    for k in range(NT):
                        sp.wait_ge(mask_done[la], (c - 1) * NS + (2 * k + 2))
                        load(k, c)

        @block.gpsimd
        def _(pool):
            pool.memset(ident[:, :], 0.0).then_inc(consts_made, 1)
            pool.memset(ones[:, :], 1.0).then_inc(consts_made, 1)
            pool.memset(ones_h[:, :], 1.0).then_inc(consts_made, 1)
            pool.memset(p_log[:, :], P_LOG).then_inc(consts_made, 1)
            pool.wait_ge(consts_made, 4)
            pool.affine_select(out=ident[:, :], in_=ident[:, :], compare_op=ALU.not_equal, fill=1.0,
                               base=0, pattern=[[-1, P]], channel_multiplier=1).then_inc(consts_made, 1)
            pool.wait_ge(h1_done, NC)
            pool.memset(src[0][:, :, 2 * F:AW], FS).then_inc(consts_made, 1)
            pool.wait_ge(flags, 1)
            with pool.If(pool.value_load(beta_big[0:1, 0:1]) == 0):
                for t in range(PAUSES):
                    pool.wait_ge(ph_done[0], t + 1)
                    wait(pool, pv_done[0], t + 1 - LAG)
                    pool.tensor_tensor(pl_ring[:, t % LAG, :], m_ring[:, t % LAG, :], ph_ring[:, t % LAG, :],
                                       ALU.subtract).then_inc(pl_early, 1)
            pool.wait_ge(xn_ready[0], NC)
            pool.wait_ge(agg_tiles, NC * NT)
            pool.memset(src[1][:, :, 2 * F:AW], FS).then_inc(consts_made, 1)

            def add_sums(la, c):
                pool.wait_ge(acc_out[la], c + 1)
                pool.tensor_tensor(t2[:, :, :], accs[:, :, 0:F], accs[:, :, F:2 * F], ALU.add)\
                    .then_inc(summed[la], 1)

            for la in range(2):
                with pool.If(pool.value_load(beta_big[0:1, la:la + 1]) != 0):
                    if la == 0:
                        pool.wait_ge(xt_lo[0], NC)
                    else:
                        pool.wait_ge(pl_done[0], NC * NS)
                        pool.wait_ge(ph_done[0], NC * NS)
                    pool.dma_start(adj_rows, adj_v[0, :, :]).then_inc(rows_in[la], 16)
                    with pool.Fori(1, NB) as b:
                        pool.wait_ge(rows_used[la], b)
                        pool.dma_start(adj_rows, adj_v[ds(b, 1), :, :].rearrange("o p j -> p (o j)"))\
                            .then_inc(rows_in[la], 16)
                with pool.Fori(0, NC) as c:
                    add_sums(la, c)
                    if la == 1:
                        pool.wait_ge(out_ready, c + 1)
                        pool.dma_start(out_v[:, ds(c * CB, CB), :], x_sb[:, ds(c * CB, CB), :]).then_inc(stored, 16)
            pool.wait_ge(stored, 16 * NC)

        @block.tensor
        def _(pe):
            pe.wait_ge(consts_made, 5)
            pe.wait_ge(embed_in, 16 * 2)

            def h_transposes(r):
                pe.wait_ge(h_ready, r + 1)
                wait(pe, ht_copied, r - 1)
                for b in range(CB):
                    last = nc.tensor.transpose(ht_ps[r % 2][:, ts(b, P)], h_sb[:, r * CB + b, :], ident[:, :])
                last.then_inc(ht_done, 1)

            h_transposes(0)
            for r in range(NC):
                if r + 1 < NC:
                    h_transposes(r + 1)
                pe.wait_ge(ht_copied, r + 1)
                wait(pe, g_copied, r - 1)
                for b in range(CB):
                    last = nc.tensor.matmul(g_ps[r % 2][:, b, :], ht_sb[:, ts(r * CB + b, P)], w1[:, 0:F],
                                            start=True, stop=True)
                last.then_inc(g_done, 1)
            pe.wait_ge(web_made, 1)
            for b in range(NB):
                last = nc.tensor.matmul(gb_ps[:, b:b + 1], ht_sb[:, ts(b, P)], web[:, :], start=True, stop=True)
            last.then_inc(gb_done, 1)
            pe.wait_ge(weights_in, 16 * 5)
            pe.wait_ge(g_copied, NC)
            for r in range(NC):
                wait(pe, h1_copied, r - 3)
                for b in range(CB):
                    last = nc.tensor.matmul(h1_ps[r % 4][:, b, :], ht_sb[:, ts(r * CB + b, P)], w1[:, F:2 * F],
                                            start=True, stop=True)
                last.then_inc(h1_done, 1)

            def layer_product(w_ps):
                for b in range(CB):
                    nc.tensor.matmul(w_ps[:, b, :], at_sb[:, ts(b, P)], w2[:, :], start=True, stop=True)
                for b in range(CB):
                    last = nc.tensor.matmul(n_ps[:, b:b + 1], at_sq[:, ts(b, P)], ones[:, 0:1],
                                            start=True, stop=True)
                last.then_inc(w_done, 1)

            def transposes(la, out_ps):
                for b in range(CB):
                    last = nc.tensor.transpose(out_ps[:, ts(b, P)], t3[:, b, :], ident[:, :])
                last.then_inc(xt_done[la], 1)

            def aggregate(c, parity, prev, prev2):
                agg = acc_ps[:, parity, :]
                for k in range(NT):
                    pe.wait_ge(tile_in[k], 16 * c + 16)
                    if prev2 and k == 0:
                        pe.wait_ge(at_ready, c - 1)
                    for b in range(TB):
                        jb = k * TB + b
                        if not prev:
                            pe.wait_ge(v_ready, jb + 1)
                        last = nc.tensor.matmul(agg, v_sb[:, jb, :], ring[:, k, b, :],
                                                start=jb == 0, stop=jb == NB - 1)
                    last.then_inc(agg_tiles, 1)
                    if prev and k == 0:
                        pe.wait_ge(at_ready, c)
                        wait(pe, w_read, c - 1)
                        layer_product(w_ps)
                    if prev2 and k == 3:
                        pe.wait_ge(xn_ready[0], c - 1)
                        transposes(0, xt_ps)

            aggregate(0, 0, False, False)
            aggregate(1, 1, True, False)
            with pe.Fori(1, NC // 2) as c2:
                aggregate(c2 * 2, 0, True, True)
                aggregate(c2 * 2 + 1, 1, True, True)

            def column_sums(la, blocks, ps):
                for jb in blocks:
                    last = nc.tensor.matmul(ps, ones_h[:, :], src[la][:, jb, :],
                                            start=jb == blocks[0], stop=jb == blocks[-1])
                last.then_inc(sums_done[la], 1)

            EARLY, LATE = range(NB - CB), range(NB - CB, NB)

            def last_products():
                pe.wait_ge(at_ready, NC)
                layer_product(w_last_ps)
                pe.wait_ge(xn_ready[0], NC - 1)
                transposes(0, xt_before_ps)

            HI, LO = 0, 1
            TAIL = (2, 1)
            PAIRS = ((HI, HI), (HI, LO), (LO, HI))

            def scores(la, c, t, shifted):
                slot_free = clamped[la] if shifted else exp_done[la]
                wait(pe, slot_free, c * NS + (t - 1))
                if shifted and t == 0:
                    pe.wait_ge(shift_ready[la], c + 1)
                for u in range(SB):
                    o = s_ps[:, t % 2, ts(u, CH)]
                    for a, b in PAIRS:
                        last = nc.tensor.matmul(o, xt[la][:, a, ts(t * SB + u, P)], xt[la][:, b, ds(c * CH, CH)],
                                                start=(a, b) == (HI, HI), stop=(a, b) == PAIRS[-1] and not shifted)
                    if shifted:
                        last = nc.tensor.matmul(o, ones[0:NB, :], neg_rows[:, :, :].rearrange("b c p -> b (c p)"),
                                                start=False, stop=True)
                last.then_inc(s_done[la], 1)

            def weighted_sum(la, c, t, joined=False):
                wait_p_lo(pe, la, c * NS + (t + 1), joined)
                if t == 0:
                    wait(pe, acc_out[la], c)
                for u in range(SB):
                    jb = t * SB + u
                    for b in range(CB):
                        col = ts(u * CB + b, P)
                        nc.tensor.matmul(acc_ps[:, b, 0:AW], ph_ring[:, t % LAG, col], src[la][:, jb, :],
                                         start=jb == 0, stop=False)
                        last = nc.tensor.matmul(acc_ps[:, b, F:AW], pl_ring[:, t % LAG, col],
                                                src[la][:, jb, F:AW], start=False, stop=jb == NB - 1)
                last.then_inc(pv_done[la], 1)

            def row_maxima(la):
                def block_row(b):
                    for j in range(NC):
                        wait(pe, sm_read[la], b * NC + j)
                        for n, (p, q) in enumerate(PAIRS):
                            last = nc.tensor.matmul(s_ps[:, 0, 0:CH], xt[la][:, p, ds(b * P, P)],
                                                    xt[la][:, q, ts(j, CH)], start=n == 0, stop=n == 2)
                        last.then_inc(sm_done[la], 1)

                block_row(0)
                with pe.Fori(1, NB) as b:
                    block_row(b)
                pe.wait_ge(neg_ready[la], 1)
                nc.tensor.transpose(s_ps[0:NB, 1, 0:P], ext[:, :], ident[:, :]).then_inc(neg_done[la], 1)
                pe.wait_ge(neg_ready[la], 2)

            def chunk(la, c, first, shifted):
                joined = la == 0 and first and not shifted
                for t in range(NS):
                    if joined and t == 1:
                        last_products()
                    if joined and t == 2:
                        column_sums(0, EARLY, early_ps)
                    if first and t == LAG:
                        pe.wait_ge(sums_out[la], 1)
                    if joined and t == LAG:
                        pe.wait_ge(w_read, NC)
                        pe.wait_ge(xt_lo[0], NC - 1)
                    if joined and t == LAST_SOURCES:
                        pe.wait_ge(exp_done[0], t - 1)
                        pe.wait_ge(xn_ready[0], NC)
                        transposes(0, slot_ps)
                    if t >= LAG:
                        weighted_sum(la, c, t - LAG, joined)
                    elif t >= TAIL[la] and not first:
                        weighted_sum(la, c - 1, NS - LAG + t)
                    if joined and t == LAST_SOURCES:
                        pe.wait_ge(xt_lo[0], NC)
                    scores(la, c, t, shifted)
                if la == 0 or first:
                    pe.wait_ge(clamped[la] if shifted else exp_done[la], c * NS + (NS - 1))
                if first:
                    column_sums(la, LATE, s_ps[:, 0, 0:AW])
                elif la == 0:
                    pe.wait_ge(xn_ready[1], c)
                    transposes(1, slot_ps)
                for t in range(TAIL[la]):
                    weighted_sum(la, c, NS - LAG + t, joined)
                if first:
                    pe.wait_ge(sums_out[la], 2)
                elif la == 0:
                    pe.wait_ge(xt_lo[1], c)

            def attention(la, shifted):
                if la == 0 and shifted:
                    last_products()
                    column_sums(0, EARLY, early_ps)
                    pe.wait_ge(xn_ready[0], NC)
                    transposes(0, slot_ps)
                    pe.wait_ge(xt_lo[0], NC)
                if shifted:
                    row_maxima(la)
                chunk(la, 0, True, shifted)
                with pe.Fori(1, NC) as c:
                    chunk(la, c, False, shifted)
                for t in range(TAIL[la], LAG):
                    weighted_sum(la, NC - 1, NS - LAG + t)
                if la == 0:
                    pe.wait_ge(consts_made, 7)
                    pe.wait_ge(acc_out[0], NC)
                    column_sums(1, EARLY, early_ps)
                    pe.wait_ge(xn_ready[1], NC)
                    transposes(1, slot_ps)

            pe.wait_ge(flags, 1)
            for la in range(2):
                if la == 0:
                    pe.wait_ge(w_read, NC - 1)
                    pe.wait_ge(xt_lo[0], NC - 2)
                else:
                    pe.wait_ge(xt_lo[1], NC)
                pe.wait_ge(consts_made, 6 + la)
                with pe.If(pe.value_load(beta_big[0:1, la:la + 1]) == 0):
                    attention(la, False)
                with pe.Else():
                    attention(la, True)

        @block.scalar
        def _(act):
            act.dma_start(w1[:, 0:F], embed).then_inc(embed_in, 16)
            act.dma_start(eb[:, :], embed_bias.rearrange("(a f) -> a f", a=1).to_broadcast([P, F]))\
                .then_inc(embed_in, 16)
            for dst, s in ((w1[:, F:2 * F], layer[0:F, :]), (w2[:, :], layer[F:2 * F, :]),
                           (lb[:, :], layer_bias.rearrange("(a f) -> a f", a=1).to_broadcast([P, F])),
                           (beta[:, 0:1], beta1.rearrange("(a f) -> a f", a=1).to_broadcast([P, 1])),
                           (beta[:, 1:2], beta2.rearrange("(a f) -> a f", a=1).to_broadcast([P, 1]))):
                act.dma_start(dst, s).then_inc(weights_in, 16)

            asks = [0, 0]

            def on(func, dst, s, **kw):
                asks[1] += 1
                act.wait_ge(asked, asks[0] + asks[1])
                nc.scalar.activation(dst, s, func, **kw).then_inc(told, 1)

            def log_terms(z, plus, minus):
                on(ACT.Ln, plus, z, bias=1.0)
                on(ACT.Ln, minus, z, bias=1.0, scale=-1.0)

            def sm(i, w):
                return small[:, i, 0:w]

            def relu(r):
                act.wait_ge(xs_ready, r + 1)
                nc.scalar.activation(h_sb[:, ts(r, CB), :], scr_b[:, ts(r, CB), :], ACT.Relu).then_inc(h_ready, 1)

            def g_out(r):
                act.wait_ge(g_done, r + 1)
                for b in range(CB):
                    q = r * CB + b
                    nc.scalar.activation(h1_sb[:, q, :], g_ps[r % 2][:, b, :], ACT.Square,
                                         accum_out=small[:, 10, q:q + 1])
                nc.scalar.activation(scr_a[:, ts(r, CB), :], g_ps[r % 2], ACT.Copy).then_inc(g_copied, 1)

            def h1_out(r):
                act.wait_ge(h1_done, r + 1)
                if r == 0:
                    act.wait_ge(g_copied, NC)
                nc.scalar.activation(h1_sb[:, ts(r, CB), :], h1_ps[r % 4], ACT.Copy).then_inc(h1_copied, 1)

            relu(0)
            for r in range(NC):
                if r + 1 < NC:
                    relu(r + 1)
                act.wait_ge(ht_done, r + 1)
                nc.scalar.activation(ht_sb[:, ds(r * CH, CH)], ht_ps[r % 2], ACT.Copy).then_inc(ht_copied, 1)
                if r:
                    g_out(r - 1)
            g_out(NC - 1)
            log_terms(sm(4, NB), sm(5, NB), sm(6, NB))
            on(ACT.Tanh, sm(5, NB), sm(4, NB))
            for r in range(NC // 2):
                h1_out(r)
            log_terms(sm(4, NB), sm(5, NB), sm(6, NB))
            for r in range(NC // 2, NC):
                h1_out(r)
            start = asks[1]

            def split_columns(la, c, ps):
                act.wait_ge(xt_done[la], c + 1)
                nc.scalar.activation(xt[la][:, 0, ds(c * CH, CH)], ps, ACT.Copy).then_inc(xt_hi[la], 1)

            def gnn_chunk(c, parity, first, pause=None):
                pause = pause or (lambda i: None)
                act.wait_ge(agg_tiles, c * NT + NT)
                if first:
                    act.wait_ge(h1_copied, NC)
                else:
                    act.wait_ge(w_done, c)
                nc.scalar.activation(at_sq, acc_ps[:, parity, :], ACT.Square)
                nc.scalar.activation(at_sb, acc_ps[:, parity, :], ACT.Copy).then_inc(at_ready, 1)
                pause(-1)
                on(ACT.Tanh, sm(5, CB), sm(4, CB))
                if c_last(c):
                    split_columns(0, c - 1, xt_before_ps)
                for i in range(4):
                    pause(i)
                log_terms(sm(4, CB), sm(5, CB), sm(6, CB))
                pause(4)
                if not first and not c_last(c):
                    split_columns(0, c - 1, xt_ps)
                on(ACT.Tanh, sm(5, CB), sm(4, CB))
                for i in (5, 6):
                    pause(i)
                on(ACT.Copy, x_sb[:, ds(c * CB, CB), :], t1[:, :, :])
                for i in range(7, PAUSES):
                    pause(i)

            def turn(c, parity, first, pause=None):
                asks[0], asks[1] = c * ASKS_CHUNK + start, 0
                gnn_chunk(c, parity, first, pause)
                assert asks[1] == ASKS_CHUNK

            turn(0, 0, True)
            turn(1, 1, False)
            with act.Fori(1, NC // 2 - 1) as c2:
                turn(c2 * 2, 0, False)
                turn(c2 * 2 + 1, 1, False)
            turn(NC - 2, 0, False)
            asks_gnn = start + NC * ASKS_CHUNK

            def exps(la, c, t, shifted):
                if shifted:
                    act.wait_ge(clamped[la], c * NS + (t + 1))
                    nc.scalar.activation(e_ring[:, t % ER, :], e_ring[:, t % ER, :], ACT.Exp,
                                         bias=p_log[:, 0:1]).then_inc(exp_done[la], 1)
                    return
                act.wait_ge(s_done[la], c * NS + (t + 1))
                wait(act, mask_done[la], c * NS + (t + 1 - ER))
                nc.scalar.activation(e_ring[:, t % ER, :], s_ps[:, t % 2, :], ACT.Exp,
                                     bias=beta_bias[:, la:la + 1], scale=beta_scale[:, la:la + 1])\
                    .then_inc(exp_done[la], 1)

            def p_hi(la, c, t):
                act.wait_ge(mask_done[la], c * NS + (t + 1))
                wait(act, pv_done[la], c * NS + (t + 1 - LAG))
                nc.scalar.activation(ph_ring[:, t % LAG, :], m_ring[:, t % LAG, :], ACT.Copy)\
                    .then_inc(ph_done[la], 1)

            def sums_leave(la, c):
                act.wait_ge(pv_done[la], c * NS + NS)
                nc.scalar.activation(accs[:, :, :], acc_ps[:, :, 0:AW], ACT.Copy).then_inc(acc_out[la], 1)

            def ask_of(la, c, n):
                act.wait_ge(asked, c * ASKS_ROWS[la] + (asks_la[la] + n + 1))

            def averages(la, c):
                ask_of(la, c, 0)
                act.wait_ge(summed[la], c + 1)
                for b in range(CB):
                    last = nc.scalar.activation(t1[:, b, :], t2[:, b, :], ACT.Copy, scale=small[:, 0, b:b + 1])
                last.then_inc(told, 1)

            def squares(c):
                ask_of(0, c, 1)
                for b in range(CB):
                    last = nc.scalar.activation(t2[:, b, :], t1[:, b, :], ACT.Square,
                                                accum_out=small[:, 2, b:b + 1])
                last.then_inc(told, 1)

            def rows_hi(c):
                nc.scalar.activation(src[1][:, ds(c * CB, CB), F:2 * F], t1[:, :, :], ACT.Copy, scale=FS)\
                    .then_inc(told, 1)

            def normalised(c):
                ask_of(0, c, 2)
                for b in range(CB):
                    last = nc.scalar.activation(t3[:, b, :], t1[:, b, :], ACT.Copy, scale=small[:, 1, b:b + 1])
                last.then_inc(xn_ready[1], 1)

            def column_sums_leave(la, part, ps):
                act.wait_ge(sums_done[la], part + 1)
                nc.scalar.activation(col_sums[:, part, :], ps, ACT.Copy).then_inc(sums_out[la], 1)

            def chunk(la, c, first, shifted, t0=0):
                for t in range(t0, NS):
                    if la == 0 and first and not shifted and t == LAST_SOURCES:
                        split_columns(0, NC - 1, slot_ps)
                    if la == 0 and not first and t == NS - 1:
                        split_columns(1, c - 1, slot_ps)
                    exps(la, c, t, shifted)
                    if la == 0 and not first and t == NS - 3:
                        normalised(c - 1)
                    if not first and t == LAG - 2:
                        sums_leave(la, c - 1)
                    if t:
                        p_hi(la, c, t - 1)
                    elif not first:
                        p_hi(la, c - 1, NS - 1)
                    if not first and t == LAG:
                        averages(la, c - 1)
                    if la == 0 and not first and t == LAG + 4:
                        squares(c - 1)
                    if la == 0 and not first and t == LAG + 5:
                        rows_hi(c - 1)
                if first:
                    column_sums_leave(la, 1, s_ps[:, 0, 0:AW])

            def between(i):
                exps(0, 0, i + 1, False)
                if i >= 0:
                    p_hi(0, 0, i)
                if i == 1:
                    column_sums_leave(0, 0, early_ps)

            def attention(la, shifted):
                if la == 0 and shifted:
                    turn(NC - 1, 1, False)
                    column_sums_leave(0, 0, early_ps)
                    split_columns(0, NC - 1, slot_ps)
                if la == 0 and not shifted:
                    turn(NC - 1, 1, False, between)
                    chunk(0, 0, True, False, PAUSES + 1)
                else:
                    chunk(la, 0, True, shifted)
                with act.Fori(1, NC) as c:
                    chunk(la, c, False, shifted)
                p_hi(la, NC - 1, NS - 1)
                sums_leave(la, NC - 1)
                averages(la, NC - 1)
                if la == 0:
                    squares(NC - 1)
                    rows_hi(NC - 1)
                    normalised(NC - 1)
                    column_sums_leave(1, 0, early_ps)
                    split_columns(1, NC - 1, slot_ps)

            asks_la = [asks_gnn, asks_gnn + NC * ASKS_ROWS[0]]
            act.wait_ge(flags, 1)
            for la in range(2):
                with act.If(act.value_load(beta_big[0:1, la:la + 1]) == 0):
                    attention(la, False)
                with act.Else():
                    attention(la, True)

        @block.vector
        def _(dve):
            step = Chain(dve, vec)
            answers, asks = [0, 0], [0]
            V = nc.vector

            def ask(ins, n=1):
                ins.then_inc(asked, n)
                asks[0] += n
                dve.wait_ge(asked, answers[0] + asks[0])

            def answered(n=1):
                answers[1] += n
                dve.wait_ge(told, answers[0] + answers[1])

            def sm(i, w):
                return small[:, i, 0:w]

            def total(dst, s):
                step(V.tensor_reduce(dst, s, axis=AX.X, op=ALU.add))

            def inv_sqrt(y, v, t):
                step(V.tensor_scalar(y.bitcast(i32), v.bitcast(i32), 1, None, ALU.logical_shift_right))
                step(V.tensor_scalar(y.bitcast(i32), y.bitcast(i32), -1.0, float(0x5F3759DF), ALU.mult, ALU.add))
                for _ in range(3):
                    step(V.tensor_tensor(t, y, y, ALU.mult))
                    step(V.scalar_tensor_tensor(t, t, -0.5, v, ALU.mult, ALU.mult))
                    step(V.scalar_tensor_tensor(y, t, 1.5, y, ALU.add, ALU.mult))

            def norm(n, rn, squares, eps, w):
                v, t = sm(14, w), sm(15, w)
                step(V.tensor_scalar(v, squares, TINY, None, ALU.max))
                inv_sqrt(rn, v, t)
                V.tensor_tensor(n, rn, v, ALU.mult)
                step(V.tensor_scalar(rn, rn, 1.0 / eps, None, ALU.min))
                step(V.tensor_scalar(n, n, eps, None, ALU.max))

            def atanh_over(c, n, rn, w):
                z, lp, lm, u, s = (sm(i, w) for i in (4, 5, 6, 7, 8))
                ask(V.tensor_scalar(z, n, MAX_TANH, None, ALU.min), 2)
                step(V.tensor_tensor(u, z, z, ALU.mult))
                step(V.tensor_scalar(s, u, 1.0 / 13, None, ALU.mult))
                for k in (11, 9, 7, 5, 3):
                    step(V.scalar_tensor_tensor(s, s, 1.0 / k, u, ALU.add, ALU.mult))
                step(V.scalar_tensor_tensor(s, s, 1.0, z, ALU.add, ALU.mult))
                answered(2)
                step(V.tensor_tensor(lp, lp, lm, ALU.subtract))
                step(V.scalar_tensor_tensor(s, lp, -0.5, s, ALU.mult, ALU.add))
                step(V.tensor_scalar(u, z, SERIES, None, ALU.is_lt))
                step(V.tensor_tensor(s, s, u, ALU.mult))
                step(V.scalar_tensor_tensor(s, lp, 0.5, s, ALU.mult, ALU.add))
                step(V.tensor_tensor(c, s, rn, ALU.mult))

            def product_scalars(nw, c, gb, ww, y, w):
                z, th, den, al, xy, x2 = (sm(i, w) for i in (4, 5, 6, 11, 12, 13))
                step(V.tensor_tensor(z, nw, c, ALU.mult))
                ask(V.tensor_scalar(z, z, EPS, None, ALU.max))
                step(V.reciprocal(al, z))
                step(V.tensor_tensor(al, al, c, ALU.mult))
                answered()
                step(V.tensor_tensor(al, al, th, ALU.mult))
                V.tensor_tensor(xy, al, gb, ALU.mult)
                step(V.tensor_tensor(x2, al, al, ALU.mult))
                V.tensor_scalar(xy, xy, 2.0, 1.0, ALU.mult, ALU.add)
                step(V.tensor_tensor(x2, x2, ww, ALU.mult))
                step(V.scalar_tensor_tensor(den, x2, y, xy, ALU.mult, ALU.add))
                step(V.tensor_scalar(den, den, EPS, None, ALU.max))
                V.scalar_tensor_tensor(xy, xy, y, al, ALU.add, ALU.mult)
                step(V.reciprocal(den, den))
                V.tensor_scalar(x2, x2, -1.0, 1.0, ALU.mult, ALU.add)
                step(V.tensor_tensor(xy, xy, den, ALU.mult))
                step(V.tensor_tensor(x2, x2, den, ALU.mult))

            def blocks(r):
                return range(r * CB, (r + 1) * CB)

            for i in range(XP):
                dve.wait_ge(x_in[i], 16)
                for b in range(i * NB // XP, (i + 1) * NB // XP):
                    ins = V.bn_stats(stats[:, b, :], x_sb[:, b, :])
                step(ins)
                V.memset(sm(0, NB), 0.0)
                for b in range(i * NB // XP, (i + 1) * NB // XP):
                    ins = V.bn_aggr(mean_var[:, b, :], stats[:, b, :])
            step(ins)
            step(V.tensor_scalar(sm(0, NB), mean_var[:, :, 1], LN_EPS, None, ALU.add))
            inv_sqrt(sm(1, NB), sm(0, NB), sm(2, NB))
            for r in range(NC):
                for b in blocks(r):
                    ins = V.tensor_scalar(scr_b[:, b, :], x_sb[:, b, :], mean_var[:, b, 0:1], small[:, 1, b:b + 1],
                                          ALU.subtract, ALU.mult)
                ins.then_inc(xs_ready, 1)
            dve.wait_ge(xs_ready, NC)
            dve.wait_ge(embed_in, 16 * 2)
            V.scalar_tensor_tensor(bsq[:, :], w1[:, 0:F], 1.0, eb[:, :], ALU.mult, ALU.mult,
                                   accum_out=web[:, :]).then_inc(web_made, 1)
            dve.wait_ge(weights_in, 16 * 5)
            for i, b in enumerate((eb, lb)):
                dve.wait_ge(web_made, i + 1)
                V.scalar_tensor_tensor(bsq[:, :], b[:, :], 1.0, b[:, :], ALU.mult, ALU.mult,
                                       accum_out=y2[:, i:i + 1]).then_inc(web_made, 1)
            for b in range(NB):
                ins = V.scalar_tensor_tensor(v_sb[:, b, :], scr_b[:, b, :], 0.0, scr_b[:, b, :],
                                             ALU.max, ALU.mult, accum_out=hh[:, b:b + 1])
            step(ins)
            norm(sm(0, NB), sm(1, NB), hh[:, :], EPS, NB)
            atanh_over(sm(2, NB), sm(0, NB), sm(1, NB), NB)
            dve.wait_ge(g_copied, NC)
            norm(sm(0, NB), sm(1, NB), sm(10, NB), EPS, NB)
            dve.wait_ge(gb_done, 1)
            product_scalars(sm(0, NB), sm(2, NB), gb_ps, sm(10, NB), y2[:, 0:1], NB)
            xy, x2, rr, cross = (sm(i, NB) for i in (12, 13, 3, 9))
            V.tensor_tensor(rr, xy, xy, ALU.mult)
            V.tensor_tensor(cross, xy, gb_ps, ALU.mult)
            step(V.tensor_scalar(sm(7, NB), x2, y2[:, 0:1], None, ALU.mult))
            V.tensor_tensor(rr, rr, sm(10, NB), ALU.mult)
            step(V.scalar_tensor_tensor(cross, cross, 2.0, sm(7, NB), ALU.mult, ALU.add))
            step(V.tensor_tensor(cross, cross, x2, ALU.mult))
            step(V.tensor_tensor(rr, rr, cross, ALU.add))
            norm(sm(0, NB), sm(1, NB), rr, EPS, NB)
            atanh_over(sm(2, NB), sm(0, NB), sm(1, NB), NB)
            V.tensor_tensor(xy, xy, sm(2, NB), ALU.mult)
            step(V.tensor_tensor(x2, x2, sm(2, NB), ALU.mult))
            V.tensor_scalar(scr_b[:, 0, :], eb[:, :], small[:, 13, 0:1], None, ALU.mult).then_inc(bias_part, 1)
            for b in range(NB):
                if b + 1 < NB:
                    V.tensor_scalar(scr_b[:, b + 1, :], eb[:, :], small[:, 13, b + 1:b + 2], None, ALU.mult)\
                        .then_inc(bias_part, 1)
                dve.wait_ge(bias_part, b + 1)
                V.scalar_tensor_tensor(v_sb[:, b, :], scr_a[:, b, :], small[:, 12, b:b + 1],
                                       scr_b[:, b, :], ALU.mult, ALU.add).then_inc(v_ready, 1)
            step(V.tensor_scalar(beta_nsign[:, :], beta[:, :], -1.0, None, ALU.mult))
            step(V.tensor_tensor(beta_abs[:, :], beta[:, :], beta_nsign[:, :], ALU.max))
            step(V.tensor_scalar(beta_scale[:, :], beta[:, :], 1.0 / FS ** 2, None, ALU.mult))
            step(V.tensor_scalar(beta_bias[:, :], beta_abs[:, :], -1.0, P_LOG, ALU.mult, ALU.add))
            step(V.tensor_scalar(beta_sign[:, :], beta[:, :], 0.0, None, ALU.is_ge))
            step(V.tensor_scalar(beta_sign[:, :], beta_sign[:, :], 2.0, -1.0, ALU.mult, ALU.add))
            step(V.tensor_scalar(beta_nsign[:, :], beta_sign[:, :], -1.0, None, ALU.mult))
            V.tensor_scalar(beta_big[:, :], beta_abs[:, :], BETA_MAX, None, ALU.is_gt).then_inc(flags, 1)
            assert asks[0] == answers[1]
            start = answers[1]
            steps_start = step.n

            def split_columns(la, c, ps):
                dve.wait_ge(xt_hi[la], c + 1)
                V.tensor_tensor(xt[la][:, 1, ds(c * CH, CH)], ps, xt[la][:, 0, ds(c * CH, CH)], ALU.subtract)\
                    .then_inc(xt_lo[la], 1)

            def gnn_chunk(c, first, pause=None):
                pause = pause or (lambda i: None)
                w_in = w_last_ps if c_last(c) else w_ps
                rows = ds(c * CB, CB)
                both, squares = slice(CB, 2 * CB), small[:, 2, 0:2 * CB]
                dve.wait_ge(w_done, c + 1)
                norm(sm(4, CB), sm(1, CB), n_ps, EPS, CB)
                ask(V.tensor_copy(sm(4, CB), sm(4, CB)))
                if c_last(c):
                    split_columns(0, c - 1, xt_before_ps)
                pause(0)
                answered()
                step(V.tensor_tensor(sm(3, CB), sm(5, CB), sm(1, CB), ALU.mult))
                for b in range(CB):
                    ins = V.scalar_tensor_tensor(t1[:, b, :], w_in[:, b, :], small[:, 3, b:b + 1],
                                                 h1_sb[:, c * CB + b, :], ALU.mult, ALU.add)
                step(ins)
                pause(1)
                V.tensor_tensor(sm(7, CB), sm(3, CB), sm(3, CB), ALU.mult)
                for b in range(CB):
                    ins = V.scalar_tensor_tensor(t2[:, b, :], t1[:, b, :], 1.0, t1[:, b, :], ALU.mult, ALU.mult,
                                                 accum_out=small[:, 2, CB + b:CB + b + 1])
                step(ins)
                V.tensor_tensor(sm(7, CB), sm(7, CB), n_ps, ALU.mult)
                for b in range(CB):
                    ins = V.scalar_tensor_tensor(t2[:, b, :], t1[:, b, :], 1.0, lb[:, :], ALU.mult, ALU.mult,
                                                 accum_out=small[:, 9, b:b + 1])
                step(ins)
                V.tensor_copy(sm(10, CB), small[:, 2, both]).then_inc(w_read, 1)
                dve.wait_ge(w_read, c + 1)
                step(V.tensor_tensor(small[:, 2, 0:CB], sm(7, CB), hh[:, rows], ALU.add))
                pause(2)
                norm(sm(0, 2 * CB), sm(1, 2 * CB), squares, EPS, 2 * CB)
                pause(3)
                atanh_over(sm(2, CB), sm(0, CB), sm(1, CB), CB)
                pause(4)
                if not first and not c_last(c):
                    split_columns(0, c - 1, xt_ps)
                product_scalars(small[:, 0, both], sm(2, CB), sm(9, CB), sm(10, CB), y2[:, 1:2], CB)
                pause(5)
                for b in range(CB):
                    ins = V.tensor_scalar(t2[:, b, :], lb[:, :], small[:, 13, b:b + 1], None, ALU.mult)
                step(ins)
                for b in range(CB):
                    ins = V.scalar_tensor_tensor(t1[:, b, :], t1[:, b, :], small[:, 12, b:b + 1], t2[:, b, :],
                                                 ALU.mult, ALU.add)
                step(ins)
                pause(6)
                ask(V.tensor_tensor(t1[:, :, :], x_sb[:, rows, :], t1[:, :, :], ALU.add))
                for b in range(CB):
                    ins = V.bn_stats(stats[:, b, :], t1[:, b, :])
                step(ins)
                pause(7)
                V.memset(sm(0, CB), 0.0)
                for b in range(CB):
                    ins = V.bn_aggr(mean_var[:, b, :], stats[:, b, :])
                step(ins)
                V.tensor_scalar(small[:, 2, 0:CB], mean_var[:, 0:CB, 1], LN_EPS, None, ALU.add)
                for b in range(CB):
                    ins = V.tensor_scalar(t2[:, b, :], t1[:, b, :], mean_var[:, b, 0:1], None, ALU.subtract)
                step(ins)
                pause(8)
                for b in range(CB):
                    ins = V.scalar_tensor_tensor(t3[:, b, :], t2[:, b, :], 0.0, t2[:, b, :], ALU.max, ALU.mult,
                                                 accum_out=small[:, 2, CB + b:CB + b + 1])
                step(ins)
                pause(9)
                step(V.tensor_scalar(squares, squares, TINY, None, ALU.max))
                inv_sqrt(sm(1, 2 * CB), squares, sm(3, 2 * CB))
                pause(10)
                for b in range(CB):
                    ins = V.tensor_scalar(t2[:, b, :], t2[:, b, :], 0.0, small[:, 1, b:b + 1], ALU.max, ALU.mult)
                step(ins)
                V.tensor_tensor(sm(0, CB), small[:, 1, both], small[:, 2, both], ALU.mult)
                step(V.tensor_scalar(src[0][:, rows, F:2 * F], t2[:, :, :], FS, None, ALU.mult))
                pause(11)
                answered()
                step(V.scalar_tensor_tensor(src[0][:, rows, 0:F], t2[:, :, :], FS, src[0][:, rows, F:2 * F],
                                            ALU.mult, ALU.subtract))
                step(V.tensor_tensor(sm(0, CB), sm(0, CB), sm(1, CB), ALU.mult))
                step(V.tensor_scalar(sm(0, CB), sm(0, CB), NORM_EPS, None, ALU.max))
                step(V.reciprocal(sm(1, CB), sm(0, CB)))
                for b in range(CB):
                    ins = V.tensor_scalar(t3[:, b, :], t2[:, b, :], small[:, 1, b:b + 1], FS, ALU.mult, ALU.mult)
                ins.then_inc(xn_ready[0], 1)

            STEPS = 82

            def gnn_turn(c, first, pause=None):
                step.base, step.n = c * STEPS + steps_start, 0
                answers[0], answers[1], asks[0] = c * ASKS_CHUNK + start, 0, 0
                gnn_chunk(c, first, pause)
                assert step.n == STEPS and answers[1] == ASKS_CHUNK, (step.n, answers[1])

            gnn_turn(0, True)
            with dve.Fori(1, NC - 1) as c:
                gnn_turn(c, False)
            steps_gnn = steps_start + NC * STEPS
            asks_gnn = start + NC * ASKS_CHUNK

            tile_base = [16 * NC * (1 + la) for la in range(2)]

            def clamp(la, c, t):
                dve.wait_ge(s_done[la], c * NS + (t + 1))
                wait(dve, mask_done[la], c * NS + (t + 1 - ER))
                V.tensor_scalar(e_ring[:, t % ER, :], s_ps[:, t % 2, :], beta_scale[:, la:la + 1], 0.0,
                                ALU.mult, ALU.min).then_inc(clamped[la], 1)

            def mask(la, c, t, joined=False):
                k, half_tile = t * SB // TB, t * SB % TB
                dve.wait_ge(exp_done[la], c * NS + (t + 1))
                if half_tile == 0:
                    dve.wait_ge(tile_in[k], 16 * c + (tile_base[la] + 16))
                wait_p_lo(dve, la, c * NS + (t + 1 - LAG), joined)
                V.scalar_tensor_tensor(m_ring[:, t % LAG, :], ring[:, k, half_tile:half_tile + SB, :]
                                       .rearrange("p b i -> p (b i)"), 0.0, e_ring[:, t % ER, :],
                                       ALU.is_gt, ALU.mult).then_inc(mask_done[la], 1)

            def p_lo(la, c, t, n=1):
                dve.wait_ge(ph_done[la], c * NS + (t + 1))
                wait(dve, pv_done[la], c * NS + (t + 1 - LAG))
                V.tensor_tensor(pl_ring[:, t % LAG, :], m_ring[:, t % LAG, :], ph_ring[:, t % LAG, :],
                                ALU.subtract).then_inc(pl_done[la], n)

            def averages(la, c):
                step.base, step.n = c * ROWS[la] + steps_la[la], 0
                den = accs[:, :, 2 * F]
                dve.wait_ge(acc_out[la], c + 1)
                V.tensor_scalar(zero[:, :], den, 0.0, None, ALU.is_equal)
                step(V.tensor_scalar(sm(1, CB), den, TINY, None, ALU.max))
                V.reciprocal(sm(0, CB), sm(1, CB)).then_inc(asked, 1)

            def mean_rows(la, c, part):
                if part == 0:
                    dve.wait_ge(told, c * TOLD_ROWS[la] + (told_la[la] + 1))
                for b in range(part * CB // 2, (part + 1) * CB // 2):
                    ins = V.scalar_tensor_tensor(t1[:, b, :], mean_row[:, :], zero[:, b:b + 1], t1[:, b, :],
                                                 ALU.mult, ALU.add)
                if part:
                    ins.then_inc(vec, 1)
                    step.n += 1

            def leaky(la, c):
                dve.wait_ge(vec, c * ROWS[la] + (steps_la[la] + step.n))
                ins = V.scalar_tensor_tensor(t1[:, :, :], t1[:, :, :], LEAK, t1[:, :, :], ALU.mult, ALU.max)
                if la == 0:
                    ins.then_inc(asked, 1)
                else:
                    step(ins)
                    rows = ds(c * CB, CB)
                    V.tensor_tensor(x_sb[:, rows, :], x_sb[:, rows, :], t1[:, :, :], ALU.add).then_inc(out_ready, 1)

            def rows_lo(c):
                rows = ds(c * CB, CB)
                dve.wait_ge(told, c * TOLD_ROWS[0] + (told_la[0] + 3))
                V.scalar_tensor_tensor(src[1][:, rows, 0:F], t1[:, :, :], FS, src[1][:, rows, F:2 * F],
                                       ALU.mult, ALU.subtract)

            NORM_PARTS = 13

            def norm_part(la_c, i):
                v, y, w = sm(2, CB), sm(1, CB), sm(3, CB)
                if i == 0:
                    dve.wait_ge(told, la_c * TOLD_ROWS[0] + (told_la[0] + 2))
                else:
                    dve.wait_ge(vec, la_c * ROWS[0] + (steps_la[0] + ROWS[0] - NORM_PARTS + 1 + i))
                if i == 0:
                    ins = V.tensor_scalar(v, v, TINY, None, ALU.max)
                elif i == 1:
                    ins = V.tensor_scalar(y.bitcast(i32), v.bitcast(i32), 1, None, ALU.logical_shift_right)
                elif i == 2:
                    ins = V.tensor_scalar(y.bitcast(i32), y.bitcast(i32), -1.0, float(0x5F3759DF),
                                          ALU.mult, ALU.add)
                elif i == NORM_PARTS - 1:
                    V.tensor_scalar(y, y, 1.0 / NORM_EPS, FS, ALU.min, ALU.mult).then_inc(asked, 1)
                    return
                elif i % 3 == 0:
                    ins = V.tensor_tensor(w, y, y, ALU.mult)
                elif i % 3 == 1:
                    ins = V.scalar_tensor_tensor(w, w, -0.5, v, ALU.mult, ALU.mult)
                else:
                    ins = V.scalar_tensor_tensor(y, w, 1.5, y, ALU.add, ALU.mult)
                ins.then_inc(vec, 1)
                step.n += 1

            ROWS = (2 + NORM_PARTS - 1, 3)
            TOLD_ROWS = (3, 1)
            steps_la = [steps_gnn, steps_gnn + NC * ROWS[0]]
            told_la = [asks_gnn, asks_gnn + NC * TOLD_ROWS[0]]

            def chunk(la, c, first, shifted, t0=0):
                for t in range(t0, NS):
                    between = la == 0 and not first
                    if la == 0 and first and not shifted and t == LAST_SOURCES:
                        split_columns(0, NC - 1, slot_ps)
                    if between and t == NS - 1:
                        split_columns(1, c - 1, slot_ps)
                    if shifted:
                        if t == 0 and not first:
                            shift_rows(la, c)
                        clamp(la, c, t)
                    mask(la, c, t, t0 > 0)
                    norm_parts = range(4 * (t - LAG - 5), min(4 * (t - LAG - 4), NORM_PARTS))\
                        if between and t >= LAG + 5 else ()
                    for i in norm_parts[0:2]:
                        norm_part(c - 1, i)
                    if t > t0:
                        p_lo(la, c, t - 1, 1 + t0 if t == t0 + 1 else 1)
                    elif not first:
                        p_lo(la, c - 1, NS - 1)
                    for i in norm_parts[2:]:
                        norm_part(c - 1, i)
                    if not first and t == LAG - 1:
                        averages(la, c - 1)
                    if not first and t in (LAG + 1, LAG + 2):
                        mean_rows(la, c - 1, t - LAG - 1)
                    if not first and t == LAG + 3:
                        leaky(la, c - 1)
                    if between and t == NS - 1:
                        rows_lo(c - 1)
                if first:
                    dve.wait_ge(sums_out[la], 2)
                    V.tensor_tensor(col_sums[:, 0, :], col_sums[:, 0, :], col_sums[:, 1, :], ALU.add)\
                        .then_inc(mean_made, 1)
                    dve.wait_ge(mean_made, 2 * la + 1)
                    V.tensor_tensor(mean_row[:, :], col_sums[:, 0, 0:F], col_sums[:, 0, F:2 * F], ALU.add)\
                        .then_inc(mean_made, 1)
                    dve.wait_ge(mean_made, 2 * la + 2)
                    V.tensor_scalar(mean_row[:, :], mean_row[:, :], 1.0 / (N * FS), None, ALU.mult)
                else:
                    assert step.n == ROWS[la], step.n

            def shift_rows(la, c):
                wait(dve, s_done[la], c * NS)
                V.tensor_tensor(neg_rows[:, :, :], neg_t[:, :].unsqueeze(1).to_broadcast([NB, CB, P]),
                                ident[0:NB, ds(c * CB, CB)].unsqueeze(2).to_broadcast([NB, CB, P]),
                                ALU.mult).then_inc(shift_ready[la], 1)

            def row_maxima(la):
                dve.wait_ge(xt_lo[la], NC)
                with dve.Fori(0, NB) as b:
                    dve.wait_ge(rows_in[la], b * 16 + 16)
                    for j in range(NC):
                        V.tensor_scalar(t1[:, :, :].rearrange("p b f -> p (b f)"), adj_rows[:, ts(j, CH)],
                                        0.0, -1e9, ALU.is_le, ALU.mult).then_inc(max_step[la], 1)
                        dve.wait_ge(max_step[la], b * (2 * NC) + (2 * j + 1))
                        dve.wait_ge(sm_done[la], b * NC + (j + 1))
                        V.scalar_tensor_tensor(t2[:, :, :].rearrange("p b f -> p (b f)"), s_ps[:, 0, 0:CH],
                                               beta_sign[:, la:la + 1], t1[:, :, :].rearrange("p b f -> p (b f)"),
                                               ALU.mult, ALU.add).then_inc(max_step[la], 1)
                        dve.wait_ge(max_step[la], b * (2 * NC) + (2 * j + 2))
                        V.tensor_reduce(ext8[:, j:j + 1], t2[:, :, :].rearrange("p b f -> p (b f)"),
                                        axis=AX.X, op=ALU.max).then_inc(sm_read[la], 1)
                    dve.wait_ge(sm_read[la], b * NC + NC)
                    V.tensor_reduce(ext[:, ds(b, 1)], ext8[:, :], axis=AX.X, op=ALU.max).then_inc(rows_used[la], 1)
                dve.wait_ge(rows_used[la], NB)
                V.tensor_scalar(ext[:, :], ext[:, :], -2.0 * FS ** 2, beta_nsign[:, la:la + 1],
                                ALU.max, ALU.mult).then_inc(neg_ready[la], 1)
                dve.wait_ge(neg_done[la], 1)
                V.tensor_copy(neg_t[:, :], s_ps[0:NB, 1, 0:P]).then_inc(neg_ready[la], 1)
                dve.wait_ge(neg_ready[la], 2)

            def between(i):
                mask(0, 0, i, True)

            def attention(la, shifted):
                if la == 0 and shifted:
                    gnn_turn(NC - 1, False)
                    split_columns(0, NC - 1, slot_ps)
                if shifted:
                    row_maxima(la)
                    shift_rows(la, 0)
                if la == 0 and not shifted:
                    gnn_turn(NC - 1, False, between)
                    chunk(0, 0, True, False, PAUSES)
                else:
                    chunk(la, 0, True, shifted)
                with dve.Fori(1, NC) as c:
                    chunk(la, c, False, shifted)
                p_lo(la, NC - 1, NS - 1)
                averages(la, NC - 1)
                mean_rows(la, NC - 1, 0)
                mean_rows(la, NC - 1, 1)
                leaky(la, NC - 1)
                if la == 0:
                    for i in range(NORM_PARTS):
                        norm_part(NC - 1, i)
                    rows_lo(NC - 1)
                    split_columns(1, NC - 1, slot_ps)

            dve.wait_ge(flags, 1)
            for la in range(2):
                with dve.If(dve.value_load(beta_big[0:1, la:la + 1]) == 0):
                    attention(la, False)
                with dve.Else():
                    attention(la, True)


def kernel(x, adj, L0_gnn_embed, L0_gnn_layer, L0_gnn_embed_bias, L0_gnn_layer_bias, L1_gnn_beta1, L1_gnn_beta2):
    import concourse.bacc as bacc
    from concourse.bass_utils import run_bass_kernel_spmd

    arrays = {"x": x, "adj": adj, "adj_t": np.asarray(adj).T, "embed": L0_gnn_embed, "layer": L0_gnn_layer,
              "embed_bias": L0_gnn_embed_bias, "layer_bias": L0_gnn_layer_bias,
              "beta1": L1_gnn_beta1, "beta2": L1_gnn_beta2}
    arrays = {f"in_{k}": np.ascontiguousarray(a) for k, a in arrays.items()}
    nc = bacc.Bacc("TRN2", target_bir_lowering=False, num_devices=1)
    args = [nc.dram_tensor(k, a.shape, mybir.dt.float32, kind="ExternalInput").ap() for k, a in arrays.items()]
    out = nc.dram_tensor("out_0", arrays["in_x"].shape, mybir.dt.float32, kind="ExternalOutput").ap()
    build(nc, *args, out)
    return run_bass_kernel_spmd(nc, [arrays], core_ids=[0]).results[0]["out_0"]
```
